# Optimizing a Trainium2 kernel written in Bass

```python
import numpy as np
import jax
import jax.numpy as jnp

def _softmax(x, axis=-1):
    return jax.nn.softmax(x, axis=axis)

def _gelu(x):
    return jax.nn.gelu(x, approximate=True)

def _silu(x):
    return jax.nn.silu(x)

def _sigmoid(x):
    return jax.nn.sigmoid(x)

def _layernorm(x, axis=-1, eps=1e-05):
    m = jnp.mean(x, axis=axis, keepdims=True)
    v = jnp.var(x, axis=axis, keepdims=True)
    return (x - m) / jnp.sqrt(v + eps)

def _scatter_add(tgt, idx, src, axis=0):
    return tgt.at[idx].add(src)

def _segment_sum(src, seg, n):
    return jax.ops.segment_sum(src, seg, n)
kernel_name = 'mk_adaln_d1_jaxref_r4_f5efcb'

def setup_inputs(seed: int=0):
    np.random.seed(seed)
    _w = jnp.asarray

    def _L0_attn_setup():
        import jax, jax.numpy as jnp
        import numpy as np
        D_MODEL = 256
        N_HEADS = 16
        D_K = D_MODEL // N_HEADS
        MAX_POS = 128
        ATT_SPAN = MAX_POS
        B, T = (4, 256)
        SCALE_FACTOR = 3

        def _heads(y):
            b, t, _ = y.shape
            return y.reshape(b, t, N_HEADS, D_K).transpose(0, 2, 1, 3)
        key = jax.random.key(seed)
        ks = jax.random.split(key, 16)
        init = lambda k, shape: jax.random.normal(k, shape, dtype=jnp.float32) * 0.02
        inp = {'x': jax.random.normal(ks[0], (B, T, D_MODEL), dtype=jnp.float32), 'Wq': init(ks[1], (D_MODEL, D_MODEL)), 'bq': jnp.zeros((D_MODEL,), jnp.float32), 'Wk': init(ks[2], (D_MODEL, D_MODEL)), 'bk': jnp.zeros((D_MODEL,), jnp.float32), 'Wv': init(ks[3], (D_MODEL, D_MODEL)), 'bv': jnp.zeros((D_MODEL,), jnp.float32), 'Wo': init(ks[4], (D_MODEL, D_MODEL)), 'bo': jnp.zeros((D_MODEL,), jnp.float32), 'Wpk': init(ks[5], (D_MODEL, D_MODEL)), 'bpk': jnp.zeros((D_MODEL,), jnp.float32), 'Wpq': init(ks[6], (D_MODEL, D_MODEL)), 'bpq': jnp.zeros((D_MODEL,), jnp.float32), 'rel_emb': init(ks[7], (2 * ATT_SPAN, D_MODEL))}
        return inp
    _L0_attn_in = _L0_attn_setup()

    def _L0_ffn_setup():
        import jax, jax.numpy as jnp
        import numpy as np
        H, I, E, K = (256, 128, 32, 8)
        B, S = (4, 256)

        def silu(x):
            return x * jax.nn.sigmoid(x)
        key = jax.random.key(seed)
        ks = jax.random.split(key, 14)

        def w(k, shape, fan_in):
            return jax.random.normal(k, shape, jnp.float32) / np.float32(np.sqrt(fan_in))
        return {'hidden_states': jax.random.normal(ks[0], (B, S, H), jnp.float32), 'Wr': w(ks[1], (H, E), H), 'br': jnp.zeros((E,), jnp.float32), 'Wg_s': w(ks[2], (H, I), H), 'bg_s': jnp.zeros((I,), jnp.float32), 'Wu_s': w(ks[3], (H, I), H), 'bu_s': jnp.zeros((I,), jnp.float32), 'Wd_s': w(ks[4], (I, H), I), 'bd_s': jnp.zeros((H,), jnp.float32), 'Wg': w(ks[5], (E, H, I), H), 'bg': jnp.zeros((E, I), jnp.float32), 'Wu': w(ks[6], (E, H, I), H), 'bu': jnp.zeros((E, I), jnp.float32), 'Wd': w(ks[7], (E, I, H), I), 'bd': jnp.zeros((E, H), jnp.float32)}
    _L0_ffn_in = _L0_ffn_setup()
    _L0_c = _w((lambda *s: np.random.randn(*s).astype(np.float32) * 0.05)(16, 256))
    _L0_wmod = _w((lambda *s: np.random.randn(*s).astype(np.float32) * 0.05)(256, 6 * 256) * 256 ** (-0.5))
    _d = {'L0_attn_x': _L0_attn_in['x'], 'L0_attn_Wq': _L0_attn_in['Wq'], 'L0_attn_bq': _L0_attn_in['bq'], 'L0_attn_Wk': _L0_attn_in['Wk'], 'L0_attn_bk': _L0_attn_in['bk'], 'L0_attn_Wv': _L0_attn_in['Wv'], 'L0_attn_bv': _L0_attn_in['bv'], 'L0_attn_Wo': _L0_attn_in['Wo'], 'L0_attn_bo': _L0_attn_in['bo'], 'L0_attn_Wpk': _L0_attn_in['Wpk'], 'L0_attn_bpk': _L0_attn_in['bpk'], 'L0_attn_Wpq': _L0_attn_in['Wpq'], 'L0_attn_bpq': _L0_attn_in['bpq'], 'L0_attn_rel_emb': _L0_attn_in['rel_emb'], 'L0_ffn_Wr': _L0_ffn_in['Wr'], 'L0_ffn_br': _L0_ffn_in['br'], 'L0_ffn_Wg_s': _L0_ffn_in['Wg_s'], 'L0_ffn_bg_s': _L0_ffn_in['bg_s'], 'L0_ffn_Wu_s': _L0_ffn_in['Wu_s'], 'L0_ffn_bu_s': _L0_ffn_in['bu_s'], 'L0_ffn_Wd_s': _L0_ffn_in['Wd_s'], 'L0_ffn_bd_s': _L0_ffn_in['bd_s'], 'L0_ffn_Wg': _L0_ffn_in['Wg'], 'L0_ffn_bg': _L0_ffn_in['bg'], 'L0_ffn_Wu': _L0_ffn_in['Wu'], 'L0_ffn_bu': _L0_ffn_in['bu'], 'L0_ffn_Wd': _L0_ffn_in['Wd'], 'L0_ffn_bd': _L0_ffn_in['bd'], 'L0_c': _L0_c, 'L0_wmod': _L0_wmod}
    _x0 = _d['L0_attn_x']
    _d['L0_attn_x'] = jax.random.normal(jax.random.fold_in(jax.random.key(seed), 1), (16, 512, 256), dtype=_x0.dtype)
    del _x0
    return _d

def reference(L0_attn_x, L0_attn_Wq, L0_attn_bq, L0_attn_Wk, L0_attn_bk, L0_attn_Wv, L0_attn_bv, L0_attn_Wo, L0_attn_bo, L0_attn_Wpk, L0_attn_bpk, L0_attn_Wpq, L0_attn_bpq, L0_attn_rel_emb, L0_ffn_Wr, L0_ffn_br, L0_ffn_Wg_s, L0_ffn_bg_s, L0_ffn_Wu_s, L0_ffn_bu_s, L0_ffn_Wd_s, L0_ffn_bd_s, L0_ffn_Wg, L0_ffn_bg, L0_ffn_Wu, L0_ffn_bu, L0_ffn_Wd, L0_ffn_bd, L0_c, L0_wmod):

    def _L0_attn_ref(x, Wq, bq, Wk, bk, Wv, bv, Wo, bo, Wpk, bpk, Wpq, bpq, rel_emb):
        import jax, jax.numpy as jnp
        import numpy as np
        D_MODEL = 256
        N_HEADS = 16
        D_K = D_MODEL // N_HEADS
        MAX_POS = 128
        ATT_SPAN = MAX_POS
        B, T = (4, 256)
        SCALE_FACTOR = 3

        def _heads(y):
            b, t, _ = y.shape
            return y.reshape(b, t, N_HEADS, D_K).transpose(0, 2, 1, 3)
        b, t, c = x.shape
        scale = 1.0 / jnp.sqrt(jnp.asarray(D_K * SCALE_FACTOR, x.dtype))
        Q = _heads(x @ Wq.T + bq)
        K = _heads(x @ Wk.T + bk)
        V = _heads(x @ Wv.T + bv)
        rel = jnp.arange(t)[None, :] - jnp.arange(t)[:, None]
        rel_pos = jnp.clip(rel + ATT_SPAN, 0, 2 * ATT_SPAN - 1)
        p2c_pos = jnp.clip(-rel + ATT_SPAN, 0, 2 * ATT_SPAN - 1)
        scores = jnp.einsum('bhqd,bhkd->bhqk', Q, K) * scale
        pos_key = (rel_emb @ Wpk.T + bpk).reshape(2 * ATT_SPAN, N_HEADS, D_K)
        c2p = jnp.einsum('bhqd,shd->bhqs', Q, pos_key) * scale
        c2p = jnp.take_along_axis(c2p, rel_pos[None, None, :, :], axis=-1)
        pos_query = (rel_emb @ Wpq.T + bpq).reshape(2 * ATT_SPAN, N_HEADS, D_K)
        p2c = jnp.einsum('bhkd,shd->bhks', K, pos_query) * scale
        p2c = jnp.take_along_axis(p2c, p2c_pos[None, None, :, :], axis=-1)
        p2c = jnp.swapaxes(p2c, -1, -2)
        scores = scores + c2p + p2c
        probs = jax.nn.softmax(scores, axis=-1)
        ctx = jnp.einsum('bhqk,bhkd->bhqd', probs, V)
        ctx = ctx.transpose(0, 2, 1, 3).reshape(b, t, c)
        return ctx @ Wo.T + bo

    def _L0_ffn_ref(hidden_states, Wr, br, Wg_s, bg_s, Wu_s, bu_s, Wd_s, bd_s, Wg, bg, Wu, bu, Wd, bd):
        import jax, jax.numpy as jnp
        import numpy as np
        H, I, E, K = (256, 128, 32, 8)
        B, S = (4, 256)

        def silu(x):
            return x * jax.nn.sigmoid(x)
        b, s, h = hidden_states.shape
        T = b * s
        x = hidden_states.reshape(T, h)
        logits = jnp.dot(x.astype(jnp.float32), Wr) + br
        aff = jax.nn.sigmoid(logits)
        top_v, top_i = jax.lax.top_k(aff, K)
        top_w = top_v / (jnp.sum(top_v, axis=-1, keepdims=True) + 1e-09)
        top_w = top_w.astype(hidden_states.dtype)
        e_total = Wr.shape[1]
        w_full = jnp.zeros((T, e_total), hidden_states.dtype)
        w_full = w_full.at[jnp.arange(T)[:, None], top_i].set(top_w)
        shared = jnp.dot(silu(jnp.dot(x, Wg_s) + bg_s) * (jnp.dot(x, Wu_s) + bu_s), Wd_s) + bd_s
        gate = silu(jnp.einsum('th,ehi->eti', x, Wg) + bg[:, None, :])
        up = jnp.einsum('th,ehi->eti', x, Wu) + bu[:, None, :]
        down = jnp.einsum('eti,eih->eth', gate * up, Wd) + bd[:, None, :]
        routed = jnp.einsum('te,eth->th', w_full, down)
        return (shared + routed).reshape(b, s, h)
    x = L0_attn_x
    mod = (_silu(L0_c) @ L0_wmod).reshape(L0_c.shape[0], 6, 1, -1)
    sa, ca, ga, sb, cb, gb = (mod[:, 0], mod[:, 1], mod[:, 2], mod[:, 3], mod[:, 4], mod[:, 5])
    ga = (2 * (ga >= 0) - 1) * jnp.maximum(jnp.abs(ga), 0.25)
    gb = (2 * (gb >= 0) - 1) * jnp.maximum(jnp.abs(gb), 0.25)
    h = _layernorm(x, axis=-1) * (1 + ca) + sa
    x = x + ga * _L0_attn_ref(h, L0_attn_Wq, L0_attn_bq, L0_attn_Wk, L0_attn_bk, L0_attn_Wv, L0_attn_bv, L0_attn_Wo, L0_attn_bo, L0_attn_Wpk, L0_attn_bpk, L0_attn_Wpq, L0_attn_bpq, L0_attn_rel_emb)
    h = _layernorm(x, axis=-1) * (1 + cb) + sb
    x = x + gb * _L0_ffn_ref(h, L0_ffn_Wr, L0_ffn_br, L0_ffn_Wg_s, L0_ffn_bg_s, L0_ffn_Wu_s, L0_ffn_bu_s, L0_ffn_Wd_s, L0_ffn_bd_s, L0_ffn_Wg, L0_ffn_bg, L0_ffn_Wu, L0_ffn_bu, L0_ffn_Wd, L0_ffn_bd)
    return x

_drawn_inputs = setup_inputs


def setup_inputs(seed=0):
    import zlib

    import numpy as np

    out = dict(_drawn_inputs(seed))
    spreads = {'L0_attn_bq': (0.0, 0.8),
     'L0_attn_bk': (0.0, 0.8),
     'L0_attn_bv': (0.0, 0.8),
     'L0_attn_bo': (0.0, 0.309),
     'L0_attn_bpk': (0.0, 0.8),
     'L0_attn_bpq': (0.0, 0.8),
     'L0_ffn_br': (0.0, 0.456),
     'L0_ffn_bg_s': (0.0, 0.528),
     'L0_ffn_bu_s': (0.0, 0.585),
     'L0_ffn_bd_s': (0.0, 0.33),
     'L0_ffn_bg': (0.0, 0.8),
     'L0_ffn_bu': (0.0, 0.8),
     'L0_ffn_bd': (0.0, 0.8)}
    factors = {'L0_attn_Wq': 8.0,
     'L0_attn_Wk': 8.0,
     'L0_attn_Wv': 8.0,
     'L0_attn_Wo': 6.294,
     'L0_attn_Wpk': 8.0,
     'L0_attn_Wpq': 8.0,
     'L0_attn_rel_emb': 8.0}
    for name, (base, spread) in spreads.items():
        noise = np.random.default_rng([zlib.crc32(name.encode()), seed]).standard_normal(out[name].shape)
        drawn = base * np.exp(spread * noise) if base else spread * noise
        out[name] = jnp.asarray(drawn.astype(out[name].dtype))
    for name, factor in factors.items():
        out[name] = (out[name] * factor).astype(out[name].dtype)
    return out
```

```python
from contextlib import ExitStack

import concourse.bass as bass
from concourse import mybir

F32 = mybir.dt.float32
F32R = mybir.dt.float32r
ALU = mybir.AluOpType
ACT = mybir.ActivationFunctionType

P = 128
B, T, D = 16, 512, 256
DC = D // P
TT = T // P
H, DK = 16, 16
PAIRS = H // 2
SPAN = 128
S = 2 * SPAN
PITCH = S + SPAN
WIN = PITCH
CSW = SPAN + T * TT + SPAN
SCALE = 1.0 / float(DK * 3) ** 0.5
E, I, TOPK = 32, 128, 8
EA = E + 1
WCOLS = 2 * DC * I + D
BLK = 1024
NBLK = B * T // BLK
EPS = 1e-5
BIG = 3.0e38
CREDIT = 16



def at(n):
    return n + CREDIT


def dma_at(n):
    return 16 * (n + CREDIT)


def credit(eng, sems, dma_sems):
    for s in sems:
        eng.sem_inc(s, CREDIT)
    for s in dma_sems:
        eng.sem_inc(s, 16 * CREDIT)


def alloc(nc, ctx):
    def sb(name, shape, dt=F32):
        return ctx.enter_context(nc.sbuf_tensor(name, shape, dt))

    def ps(name, shape=(P, 512)):
        return ctx.enter_context(nc.psum_tensor(name, list(shape), F32))

    def sem(name):
        return ctx.enter_context(nc.semaphore(name))

    return sb, ps, sem


def build_setup(nc, d):
    with ExitStack() as ctx:
        sb, ps, sem = alloc(nc, ctx)
        ident = sb("su_ident", [P, P])
        cT = sb("su_cT", [P, DC, B])
        sig = sb("su_sig", [P, DC, B])
        silu = sb("su_silu", [P, DC, B])
        wmod = sb("su_wmod", [P, DC, 6 * D])
        rows = sb("su_rows", [B, 6 * D])
        sgn = sb("su_sgn", [B, D])
        mag = sb("su_mag", [B, D])
        cols = sb("su_cols", [P, B, 6, DC])
        csgn = sb("su_csgn", [P, B, DC])
        cmag = sb("su_cmag", [P, B, DC])
        rel = sb("su_rel", [P, DC, 2, S])
        wpk = sb("su_wpk", [P, DC, PAIRS * P])
        wpq = sb("su_wpq", [P, DC, PAIRS * P])
        wpos = sb("su_wpos", [P, DC, 2 * D])
        bpos = sb("su_bpos", [P, 2, PAIRS])
        bqk = sb("su_bqk", [P, 4, 2])
        basis = sb("su_basis", [P, 4])
        fsel = sb("su_fsel", [P, P])
        rmask = sb("su_rmask", [P, 4])
        raw = sb("su_raw", [P, 3, S])
        delta = sb("su_delta", [P, 3, S])
        nega = sb("su_nega", [P, 2])
        fl = sb("su_fl", [P, 2, P])
        full = sb("su_full", [P, S])
        part = sb("su_part", [P, 2, S], F32R)
        tab = sb("su_tab", [P, 2, 2, S])
        zero = sb("su_zero", [P, 3072])
        p_a, p_b = ps("su_pa"), ps("su_pb")
        p_t = [ps(f"su_pt{i}") for i in range(4)]
        loaded = sem("su_loaded")
        zeroed, zdone = sem("su_zeroed"), sem("su_zdone")
        exp_done = sem("su_exp")
        step = sem("su_step")
        modp = sem("su_modp")
        tabp = sem("su_tabp")
        biased = sem("su_biased")
        tab_ready, stored, fp = sem("su_tab_ready"), [sem("su_st0"), sem("su_st1")], sem("su_fp")
        mod_st = sem("su_modst")
        fsum = sem("su_fsum")
        block = ctx.enter_context(nc.Block())
        marks = {}

        @block.sync
        def _(sp):
            sp.dma_start(cT[:, :, :], d["cT"].rearrange("(c p) b -> p c b", p=P)).then_inc(loaded, 16)
            sp.dma_start(wmod[:, :, :], d["wmod"].rearrange("(c p) n -> p c n", p=P)).then_inc(loaded, 16)
            sp.dma_start(rel[:, :, 0, :], d["relT"].rearrange("(c p) n -> p c n", p=P)).then_inc(loaded, 16)
            sp.dma_start(rel[:, :, 1, :], d["relTr"].rearrange("(c p) n -> p c n", p=P)).then_inc(loaded, 16)
            sp.dma_start(wpk[:, :, :], d["wpk"].rearrange("(c p) n -> p c n", p=P)).then_inc(loaded, 16)
            sp.dma_start(wpq[:, :, :], d["wpq"].rearrange("(c p) n -> p c n", p=P)).then_inc(loaded, 16)
            sp.dma_start(bpos[:, :, :], d["bpos"]).then_inc(loaded, 16)
            sp.dma_start(fsel[:, :], d["fsel"]).then_inc(loaded, 16)
            sp.dma_start(rmask[:, :], d["rowmask"]).then_inc(loaded, 16)
            sp.dma_start(bqk[:, :, :], d["bqk"]).then_inc(loaded, 16)
            sp.dma_start(wpos[:, :, :], d["wpos"].rearrange("(c p) n -> p c n", p=P)).then_inc(loaded, 16)
            sp.dma_start(d["headpad"], d["pad"]).then_inc(zdone, 16)
            sp.wait_ge(zeroed, 1)
            n = 16
            for t in ("scrC", "scrP"):
                for i in range(2):
                    size = d[t].shape[1] - 2 * P
                    sp.dma_start(d[t][i, 0:size].rearrange("(p n) -> p n", p=P),
                                 zero[:, 0:size // P]).then_inc(zdone, 16)
                    sp.dma_start(d[t][i, size:size + 2 * P].rearrange("(p n) -> p n", p=P),
                                 zero[:, 0:2]).then_inc(zdone, 16)
                    n += 32
            for g in range(PAIRS):
                sp.wait_ge(tab_ready, g + 1)
                sp.dma_start(d["tabs"][g], tab[:, g % 2, :, :]).then_inc(stored[g % 2], 16)
            sp.wait_ge(zdone, n)
            for s in stored:
                sp.wait_ge(s, 16 * PAIRS // 2)

        @block.gpsimd
        def _(pool):
            nc.gpsimd.memset(zero[:, :], 0.0).then_inc(zeroed, 1)

        @block.scalar
        def _(act):
            act.wait_ge(loaded, 16 * 11)
            nc.scalar.activation(sig[:, :, :], cT[:, :, :], ACT.Exp, scale=-1.0).then_inc(exp_done, 1)
            for g in range(PAIRS):
                act.wait_ge(tabp, g + 1)
                if g:
                    act.wait_ge(fsum, g)
                for i in range(3):
                    kind = 0 if i == 0 else 1
                    a = nc.scalar.activation(raw[:, i, :], p_t[i][:, 0:S], ACT.Identity,
                                             bias=bpos[:, kind, g:g + 1])
                    a.then_inc(biased, 1)
            act.wait_ge(mod_st, 2)
            act.dma_start(d["modrow"], rows[:, :]).then_inc(zeroed, 16)
            act.dma_start(d["modcol"], cols[:, :, :, :]).then_inc(zeroed, 16)
            act.wait_ge(zeroed, 33)

        @block.vector
        def _(dve):
            done = [0]

            def link(ins):
                done[0] += 1
                ins.then_inc(step, 1)
                dve.wait_ge(step, done[0])

            dve.wait_ge(exp_done, 1)
            link(nc.vector.tensor_scalar_add(sig[:, :, :], sig[:, :, :], 1.0))
            link(nc.vector.reciprocal(sig[:, :, :], sig[:, :, :]))
            link(nc.vector.tensor_tensor(silu[:, :, :], sig[:, :, :], cT[:, :, :], ALU.mult))
            marks["silu"] = done[0]
            for n in range(3):
                dve.wait_ge(modp, n + 1)
                link(nc.vector.tensor_copy(rows[:, n * 512:(n + 1) * 512], p_a[0:B, :]))
                marks["row", n] = done[0]
            for k in (2, 5):
                g = rows[:, k * D:(k + 1) * D]
                link(nc.vector.tensor_scalar(sgn[:, :], g, 0.0, 2.0, ALU.is_ge, ALU.mult))
                link(nc.vector.tensor_scalar(mag[:, :], g, -1.0, None, ALU.mult))
                link(nc.vector.tensor_tensor(mag[:, :], g, mag[:, :], ALU.max))
                link(nc.vector.tensor_scalar(mag[:, :], mag[:, :], 0.25, None, ALU.max))
                link(nc.vector.scalar_tensor_tensor(out=g, in0=sgn[:, :], scalar=-1.0, in1=mag[:, :],
                                                    op0=ALU.add, op1=ALU.mult))
            nc.vector.tensor_copy(sgn[:, 0:1], mag[:, 0:1]).then_inc(mod_st, 1)
            dve.wait_ge(modp, 4)
            src = p_b[:, 0:6 * DC * B].rearrange("p (k c b) -> p b k c", k=6, c=DC)
            link(nc.vector.tensor_copy(cols[:, :, :, :], src))
            for k in (1, 4):
                link(nc.vector.tensor_scalar_add(cols[:, :, k, :], cols[:, :, k, :], 1.0))
            g, cs, cm = cols[:, :, 5, :], csgn[:, :, :], cmag[:, :, :]
            link(nc.vector.tensor_scalar(cs, g, 0.0, 2.0, ALU.is_ge, ALU.mult))
            link(nc.vector.tensor_scalar(cm, g, -1.0, None, ALU.mult))
            link(nc.vector.tensor_tensor(cm, g, cm, ALU.max))
            link(nc.vector.tensor_scalar(cm, cm, 0.25, None, ALU.max))
            link(nc.vector.scalar_tensor_tensor(out=g, in0=cs, scalar=-1.0, in1=cm, op0=ALU.add, op1=ALU.mult))
            nc.vector.tensor_copy(mag[:, 0:1], sgn[:, 0:1]).then_inc(mod_st, 1)

            dve.wait_ge(modp, 5)
            dve.wait_ge(loaded, 16 * 11)
            link(nc.vector.tensor_tensor(basis[:, :], p_a[:, 0:4], bqk[:, :, 0], ALU.add))
            link(nc.vector.tensor_tensor(d["qkbias"][:, :], basis[:, :], bqk[:, :, 1], ALU.add))

            for g in range(PAIRS):
                dve.wait_ge(biased, 3 * (g + 1))
                base = [raw[:, 0, S - 1:S], raw[:, 1, S - 1:S], raw[:, 2, 0:1]]
                for i in range(3):
                    link(nc.vector.tensor_scalar(delta[:, i, :], raw[:, i, :], base[i], None, ALU.subtract))
                link(nc.vector.tensor_scalar(nega[:, 0:1], base[1], -1.0, None, ALU.mult))
                link(nc.vector.tensor_scalar(nega[:, 1:2], base[0], -1.0, None, ALU.mult))
                if g == 0:
                    dve.wait_ge(loaded, 16 * 11)
                for i in range(2):
                    link(nc.vector.tensor_scalar(fl[:, i, :], fsel[:, :], nega[:, i:i + 1], None, ALU.mult))
                marks["delta", g] = done[0]
                dve.wait_ge(fp, g + 1)
                link(nc.vector.tensor_tensor(full[:, :], p_t[3][:, 0:S], delta[:, 0, :], ALU.add))
                if g >= 2:
                    dve.wait_ge(stored[g % 2], 16 * (g // 2))
                for i, src in ((0, full[:, :]), (1, delta[:, 2, :])):
                    link(nc.vector.tensor_scalar(part[:, i, :], src, rmask[:, 2 * i:2 * i + 1], None, ALU.mult))
                    ins = nc.vector.scalar_tensor_tensor(
                        out=tab[:, g % 2, i, :], in0=src, scalar=rmask[:, 2 * i + 1:2 * i + 2],
                        in1=part[:, i, :].bitcast(F32), op0=ALU.mult, op1=ALU.add)
                    link(ins)
                nc.vector.tensor_copy(nega[:, 0:1], nega[:, 1:2]).then_inc(tab_ready, 1)
                nc.vector.tensor_copy(fl[:, 0, 0:1], fl[:, 1, 0:1]).then_inc(fsum, 1)
                dve.wait_ge(fsum, g + 1)
                dve.wait_ge(tab_ready, g + 1)

        @block.tensor
        def _(pe):
            pe.wait_ge(loaded, 16 * 11)
            pe.wait_ge(step, marks["silu"])
            for n in range(3):
                if n:
                    pe.wait_ge(step, marks["row", n - 1])
                for c in range(DC):
                    m = nc.tensor.matmul(p_a[0:B, :], silu[:, c, :], wmod[:, c, n * 512:(n + 1) * 512],
                                         start=c == 0, stop=c == DC - 1)
                m.then_inc(modp, 1)
            for n in range(6 * DC):
                for c in range(DC):
                    m = nc.tensor.matmul(p_b[:, n * B:(n + 1) * B], wmod[:, c, n * P:(n + 1) * P], silu[:, c, :],
                                         start=c == 0, stop=c == DC - 1)
            m.then_inc(modp, 1)
            pe.wait_ge(step, marks["row", 2])
            for n in range(4):
                for c in range(DC):
                    m = nc.tensor.matmul(p_a[:, n:n + 1], wpos[:, c, n * P:(n + 1) * P], rel[:, c, 0, S - 1:S],
                                         start=c == 0, stop=c == DC - 1)
            m.then_inc(modp, 1)
            for g in range(PAIRS):
                if g:
                    pe.wait_ge(biased, 3 * g)
                for i, w, r in ((0, wpk, 0), (1, wpq, 0), (2, wpq, 1)):
                    for c in range(DC):
                        m = nc.tensor.matmul(p_t[i][:, 0:S], w[:, c, g * P:(g + 1) * P], rel[:, c, r, :],
                                             start=c == 0, stop=c == DC - 1)
                m.then_inc(tabp, 1)
                pe.wait_ge(step, marks["delta", g])
                nc.tensor.matmul(p_t[3][:, 0:S], fl[:, 0, :], delta[:, 0, :], start=True, stop=False)
                nc.tensor.matmul(p_t[3][:, 0:S], fl[:, 1, :], delta[:, 1, :], start=False,
                                 stop=True).then_inc(fp, 1)


def build_qkv(nc, d):
    with ExitStack() as ctx:
        sb, ps, sem = alloc(nc, ctx)
        ident = sb("qk_ident", [P, P])
        w_raw = sb("qk_wraw", [P, 3, DC, D])
        w_hi = sb("qk_whi", [P, 3, DC, D], F32R)
        w_lo = sb("qk_wlo", [P, 3, DC, D], F32R)
        bv = sb("qk_bv", [P, D])
        mod = sb("qk_mod", [P, B * 6 * DC])
        mb = sb("qk_mb", [P, 6, DC])
        xt = [sb(f"qk_x{u}", [P, TT, D]) for u in range(2)]
        st = sb("qk_st", [P, TT, 6])
        mv = sb("qk_mv", [P, TT, 2])
        rstd = sb("qk_rstd", [P, TT])
        power = sb("qk_power", [P, TT])
        var = sb("qk_var", [P, TT])
        hn = sb("qk_hn", [P, TT, D])
        hT = sb("qk_hT", [P, DC, T])
        h_hi = sb("qk_hhi", [P, DC, T], F32R)
        h_lo = sb("qk_hlo", [P, DC, T], F32R)
        q_hi = sb("qk_qhi", [P, 4, T], F32R)
        q_lo = sb("qk_qlo", [P, 4, T], F32R)
        v = sb("qk_v", [P, TT, D])
        p_h = [ps(f"qk_ph{c}") for c in range(DC)]
        p_q = [ps(f"qk_pq{i}") for i in range(4)]
        p_v = [ps(f"qk_pv{i}") for i in range(2)]
        loaded, wsplit, power_set = sem("qk_loaded"), sem("qk_wsplit"), sem("qk_power_set")
        x_in = [sem("qk_xin0"), sem("qk_xin1")]
        stats = sem("qk_stats")
        powered, normed, transposed = sem("qk_powered"), sem("qk_normed"), sem("qk_transposed")
        modulated, split, projected, vprod = (sem("qk_modulated"), sem("qk_split"), sem("qk_projected"),
                                              sem("qk_vprod"))
        hi_ready, lo_ready, v_ready = sem("qk_hi"), sem("qk_lo"), sem("qk_v_ready")
        stored = sem("qk_stored")
        STATS = 2 * TT + 2
        STORES = 13
        block = ctx.enter_context(nc.Block())

        @block.sync
        def _(sp):
            credit(sp, [stats, powered, normed, transposed, modulated, split, projected, vprod,
                        hi_ready, lo_ready, v_ready], [stored])
            for u in range(2):
                sp.dma_start(xt[u][:, :, :], d["x"][u].rearrange("(t p) n -> p t n", p=P)).then_inc(x_in[u], 16)
            for i, w in enumerate(("wq", "wk", "wv")):
                sp.dma_start(w_raw[:, i, :, :], d[w].rearrange("(c p) n -> p c n", p=P)).then_inc(loaded, 16)
            sp.dma_start(bv[:, :], d["bv"].partition_broadcast(P)).then_inc(loaded, 16)
            sp.dma_start(mod[:, :], d["modcol"].rearrange("p b k c -> p (b k c)")).then_inc(loaded, 16)
            sp.dma_start(ident[:, :], d["ident"]).then_inc(loaded, 16)
            with sp.Fori(0, B // 2) as bb:
                for u in range(2):
                    b = bb * 2 + u
                    sp.wait_ge(normed, at(TT * b + TT))
                    sp.dma_start(xt[u][:, :, :], d["x"][bass.ds((b + 2) % B, 1)].squeeze(0)
                                 .rearrange("(t p) n -> p t n", p=P)).then_inc(x_in[u], 16)
                    sp.wait_ge(hi_ready, at(b * 4 + 4))
                    sp.wait_ge(lo_ready, at(b * 4 + 4))
                    for i in range(4):
                        parts = (q_hi, q_lo, q_hi) if i < 2 else (q_hi, q_hi, q_lo)
                        dst = d["stackQ" if i < 2 else "stackK"]
                        for k, src in enumerate(parts):
                            o = dst[bass.ds(b * H + 8 * (i % 2), 8), k]
                            sp.dma_start(o, src[:, i, :].bitcast(F32)).then_inc(stored, 16)
                    sp.wait_ge(v_ready, at(b * TT + TT))
                    sp.dma_start(d["vals"][bass.ds(b, 1)].squeeze(0), v[:, :, :]).then_inc(stored, 16)
            sp.wait_ge(stored, dma_at(STORES * B))
            for u in range(2):
                sp.wait_ge(x_in[u], 16 * (B // 2 + 1))

        @block.gpsimd
        def _(pool):
            nc.gpsimd.memset(power[:, :], -0.5).then_inc(power_set, 1)
            pool.wait_ge(power_set, 1)
            with pool.Fori(0, B) as b:
                pool.wait_ge(stats, at(b * STATS + STATS))
                pool.wait_ge(normed, at(b * TT))
                nc.gpsimd.tensor_tensor(rstd[:, :], var[:, :], power[:, :], ALU.pow).then_inc(powered, 1)

        @block.scalar
        def _(act):
            with act.Fori(0, B) as b:
                act.wait_ge(transposed, at(b + 1))
                act.wait_ge(split, at(b * 4))
                for c in range(DC):
                    nc.scalar.activation(hT[:, c, :], p_h[c][:, :], ACT.Identity, scale=mb[:, 1, c:c + 1],
                                         bias=mb[:, 0, c:c + 1]).then_inc(modulated, 1)
                act.wait_ge(stored, dma_at(b * STORES))
                for i in range(4):
                    act.wait_ge(projected, at(b * 4 + i + 1))
                    nc.scalar.activation(q_hi[:, i, :], p_q[i][:, :], ACT.Identity,
                                         bias=d["qkbias"][:, i:i + 1]).then_inc(hi_ready, 1)

        @block.vector
        def _(dve):
            dve.wait_ge(loaded, 16 * 6)
            nc.vector.tensor_copy(w_hi[:, :, :, :], w_raw[:, :, :, :]).then_inc(wsplit, 1)
            dve.wait_ge(wsplit, 1)
            nc.vector.tensor_tensor(w_lo[:, :, :, :], w_raw[:, :, :, :], w_hi[:, :, :, :].bitcast(F32),
                                    ALU.subtract).then_inc(wsplit, 1)
            with dve.Fori(0, B // 2) as bb:
                for u in range(2):
                    b = bb * 2 + u
                    dve.wait_ge(x_in[u], bb * 16 + 16)
                    for t in range(TT):
                        nc.vector.bn_stats(st[:, t, :], xt[u][:, t, :]).then_inc(stats, 1)
                    dve.wait_ge(modulated, at(b * DC))
                    dve.wait_ge(stats, at(b * STATS + TT))
                    nc.vector.tensor_copy(mb[:, :, :], mod[:, bass.ds(b * (6 * DC), 6 * DC)]
                                          .rearrange("p (k c) -> p k c", c=DC)).then_inc(stats, 1)
                    for t in range(TT):
                        nc.vector.bn_aggr(mv[:, t, :], st[:, t, :]).then_inc(stats, 1)
                    dve.wait_ge(stats, at(b * STATS + 1 + 2 * TT))
                    nc.vector.tensor_scalar_add(var[:, :], mv[:, :, 1], EPS).then_inc(stats, 1)
                    dve.wait_ge(powered, at(b + 1))
                    dve.wait_ge(transposed, at(b))
                    for t in range(TT):
                        nc.vector.tensor_scalar(hn[:, t, :], xt[u][:, t, :], mv[:, t, 0:1], rstd[:, t:t + 1],
                                                ALU.subtract, ALU.mult).then_inc(normed, 1)
                    dve.wait_ge(vprod, at(b * TT))
                    dve.wait_ge(projected, at(b * 4))
                    for c in range(DC):
                        dve.wait_ge(modulated, at(b * DC + c + 1))
                        nc.vector.tensor_copy(h_hi[:, c, :], hT[:, c, :]).then_inc(split, 1)
                    dve.wait_ge(split, at(b * 4 + 2))
                    for c in range(DC):
                        nc.vector.tensor_tensor(h_lo[:, c, :], hT[:, c, :], h_hi[:, c, :].bitcast(F32),
                                                ALU.subtract).then_inc(split, 1)
                    dve.wait_ge(stored, dma_at(b * STORES))
                    for i in range(4):
                        dve.wait_ge(hi_ready, at(b * 4 + i + 1))
                        nc.vector.scalar_tensor_tensor(
                            out=q_lo[:, i, :], in0=p_q[i][:, :], scalar=d["qkbias"][:, i:i + 1],
                            in1=q_hi[:, i, :].bitcast(F32), op0=ALU.add, op1=ALU.subtract).then_inc(lo_ready, 1)
                    for t in range(TT):
                        dve.wait_ge(vprod, at(b * TT + 2 * (t // 2) + 2))
                        nc.vector.tensor_tensor(v[:, t, :], p_v[t // 2][:, (t % 2) * D:(t % 2) * D + D],
                                                bv[:, :], ALU.add).then_inc(v_ready, 1)

        @block.tensor
        def _(pe):
            pe.wait_ge(loaded, 16 * 6)
            pe.wait_ge(wsplit, 2)
            with pe.Fori(0, B) as b:
                pe.wait_ge(modulated, at(b * DC))
                for t in range(TT):
                    pe.wait_ge(normed, at(b * TT + t + 1))
                    for c in range(DC):
                        m = nc.tensor.transpose(p_h[c][:, t * P:(t + 1) * P], hn[:, t, c * P:(c + 1) * P],
                                                ident[:, :])
                m.then_inc(transposed, 1)
                pe.wait_ge(split, at(b * 4 + 4))
                for i in range(4):
                    pe.wait_ge(lo_ready, at(b * 4))
                    n0 = (i % 2) * P
                    prods = [(w, h, c) for w, h in ((w_hi, h_hi), (w_hi, h_lo), (w_lo, h_hi))
                             for c in range(DC)]
                    for n, (w, h, c) in enumerate(prods):
                        m = nc.tensor.matmul(p_q[i][:, :], w[:, i // 2, c, n0:n0 + P], h[:, c, :],
                                             start=n == 0, stop=n == len(prods) - 1)
                    m.then_inc(projected, 1)
                pe.wait_ge(v_ready, at(b * TT))
                for t in range(TT):
                    prods = [(w, h, c) for w, h in ((w_hi, h_hi), (w_hi, h_lo), (w_lo, h_hi))
                             for c in range(DC)]
                    for n, (w, h, c) in enumerate(prods):
                        m = nc.tensor.matmul(p_v[t // 2][:, (t % 2) * D:(t % 2) * D + D],
                                             h[:, c, t * P:(t + 1) * P], w[:, 2, c, :],
                                             start=n == 0, stop=n == len(prods) - 1)
                    m.then_inc(vprod, 1)


def build_attention(nc, d):
    with ExitStack() as ctx:
        sb, ps, sem = alloc(nc, ctx)
        TURNS = B * H // 4
        HPT = 4
        TILES = HPT * TT
        ident = sb("at_ident", [P, P])
        tri = sb("at_tri", [P, 2, P])
        ones = sb("at_ones", [P, 2 * P])
        tri_val = sb("at_tri_val", [P, 2, TT - 1, P])
        stQ = [sb(f"at_stQ{u}", [P, T], F32R) for u in range(2)]
        stK = [sb(f"at_stK{u}", [P, T], F32R) for u in range(2)]
        tab = [sb(f"at_tab{u}", [P, 2, S], F32R) for u in range(2)]
        val = [sb(f"at_val{u}", [P, TT, 2 * DK]) for u in range(2)]
        genC = [sb(f"at_genC{i}", [P, TT, S]) for i in range(2)]
        genP = [sb(f"at_genP{i}", [P, TT, S]) for i in range(2)]
        CS = [sb(f"at_CS{i}", [P, CSW]) for i in range(HPT)]
        PS = [sb(f"at_PS{i}", [P, CSW]) for i in range(HPT)]
        scores = [sb(f"at_scores{i}", [P, T]) for i in range(2)]
        probs = [sb(f"at_probs{i}", [P, T]) for i in range(2)]
        probsT = [sb(f"at_probsT{i}", [P, TT, P]) for i in range(2)]
        negmax = sb("at_negmax", [P, TT])
        sums = [sb(f"at_sums{i}", [P, TT]) for i in range(2)]
        inv = sb("at_inv", [P, TT])
        cx = sb("at_cx", [P, TT, HPT * DK])
        b_C, b_P = ps("at_bC"), ps("at_bP")
        b_S = [ps(f"at_bS{i}") for i in range(2)]
        b_T = [ps(f"at_bT{i}") for i in range(2)]
        b_X = [ps(f"at_bX{i}") for i in range(2)]
        consts, cleared = sem("at_consts"), sem("at_cleared")
        stack_in = [sem(f"at_stack_in{u}") for u in range(2)]
        val_in = [sem(f"at_val_in{u}") for u in range(2)]
        c_made, p_made, c_out, p_out = sem("at_c_made"), sem("at_p_made"), sem("at_c_out"), sem("at_p_out")
        written = [sem(f"at_written{i}") for i in range(2)]
        sheared = [sem(f"at_sheared{i}") for i in range(HPT)]
        fixed, tri_made = sem("at_fixed"), sem("at_tri_made")
        scored, biased, exped, turned = sem("at_scored"), sem("at_biased"), sem("at_exped"), sem("at_turned")
        copiedA, copiedV, summed, inverted, headed = (sem("at_copiedA"), sem("at_copiedV"), sem("at_summed"),
                                                      sem("at_inverted"), sem("at_headed"))
        ctx_out = sem("at_ctx_out")
        settled = sem("at_settled")
        STACK = 5
        block = ctx.enter_context(nc.Block())

        def gen_of(n):
            return (n // 2) % 2, slice(64 * (n % 2), 64 * (n % 2) + 64)

        def col(row_block, k):
            return SPAN + row_block * T + k

        def steps():
            for k in range(TILES + TT):
                yield (k, k if k < TILES else None,
                       (k % TT - 1) if k < TILES and k % TT in (1, 2) else None,
                       k - 2 if 2 <= k < TILES + 2 else None,
                       k - 3 if 3 <= k < TILES + 3 else None,
                       k // TT - 1 if k % TT == 3 and k >= 7 else None)

        @block.sync
        def _(sp):
            credit(sp, [c_made, p_made, c_out, p_out, fixed, tri_made, scored, biased, exped, turned, copiedA, copiedV,
                        summed, inverted, headed], stack_in + val_in + written + sheared + [ctx_out])
            sp.dma_start(ident[:, :], d["ident"]).then_inc(consts, 16)
            sp.dma_start(tri[:, :, :], d["tri"]).then_inc(consts, 16)
            sp.wait_ge(cleared, 1)
            for u in range(2):
                for j in range(2):
                    sp.dma_start(stQ[u][64 * j + 48:64 * j + 64, :].bitcast(F32), d["headpad"]).then_inc(consts, 16)

            def load_stacks(pair, u):
                for dst, src in ((stQ, "stackQ"), (stK, "stackK")):
                    for j in range(2):
                        sp.dma_start(dst[u][64 * j:64 * j + 48, :].bitcast(F32),
                                     d[src][bass.ds(2 * pair + j, 1)].rearrange("a k r t -> (a k r) t"))\
                            .then_inc(stack_in[u], 16)
                sp.dma_start(tab[u][:, :, :].bitcast(F32), d["tabs"][bass.ds(pair % PAIRS, 1)].squeeze(0))\
                    .then_inc(stack_in[u], 16)

            def load_vals(pair, u):
                sp.dma_start(val[u][:, :, :], d["vals"][bass.ds(pair // PAIRS, 1)].squeeze(0)
                             [:, :, bass.ds(pair % PAIRS * (2 * DK), 2 * DK)]).then_inc(val_in[u], 16)

            def shear(it, n):
                m = it * HPT + n
                i, cs = n % 2, n % HPT
                size = TT * P * PITCH
                sp.wait_ge(c_out, at(2 * m + 2))
                sp.wait_ge(p_out, at(2 * m + 2))
                for t, src in (("scrC", genC), ("scrP", genP)):
                    sp.dma_start(d[t][i, P:P + size].rearrange("(t p n) -> p t n", p=P, n=PITCH)[:, :, 0:S],
                                 src[i][:, :, :]).then_inc(written[i], 16)
                sp.wait_ge(written[i], dma_at(2 * (m // 2 + 1)))
                sp.wait_ge(biased, at(TT * (m - HPT + 1)))
                for k, (t, dst) in enumerate((("scrC", CS), ("scrP", PS))):
                    a = d[t][i, P - k:P - k + size]
                    src = bass.AP(a.tensor, a.offset, [[PITCH - 1, P], [P * PITCH, TT], [1, WIN]])
                    b = dst[cs][:, :]
                    sp.dma_start(bass.AP(b.tensor, b.offset, [list(b.ap[0]), [T + SPAN, TT], [1, WIN]]),
                                 src).then_inc(sheared[cs], 16)

            for u in range(2):
                load_stacks(u, u)
                load_vals(u, u)
            for n in range(2):
                shear(0, n)
            with sp.Fori(0, TURNS) as it:
                for n in range(HPT):
                    shear(it, n + 2)
                    if n % 2 == 0:
                        continue
                    u = n // 2
                    nxt = (2 * it + 2 + u) % (B * PAIRS)
                    sp.wait_ge(scored, at(it * TILES + 8 * (u + 1)))
                    load_stacks(nxt, u)
                    sp.wait_ge(summed, at(it * TILES + 8 * (u + 1)))
                    load_vals(nxt, u)
                sp.wait_ge(headed, at(it * HPT + HPT))
                sp.dma_start(d["ctxd"][bass.ds(it // 4, 1)].squeeze(0)[:, :, bass.ds(it % 4 * (HPT * DK), HPT * DK)],
                             cx[:, :, :]).then_inc(ctx_out, 16)
            for u in range(2):
                sp.wait_ge(stack_in[u], dma_at(STACK * (TURNS + 1)))
                sp.wait_ge(val_in[u], dma_at(TURNS + 1))
            sp.wait_ge(ctx_out, dma_at(TURNS))
            for cs in range(HPT):
                sp.wait_ge(sheared[cs], dma_at(2 * (TURNS + (cs < 2))))

        @block.gpsimd
        def _(pool):
            for cs in range(HPT):
                nc.gpsimd.memset(CS[cs][:, :], 0.0)
            nc.gpsimd.memset(ones[:, :], 1.0)
            for u in range(2):
                nc.gpsimd.memset(stQ[u][:, :].bitcast(F32), 0.0)
                m = nc.gpsimd.memset(stK[u][:, :].bitcast(F32), 0.0)
            m.then_inc(cleared, 1)
            pool.wait_ge(consts, 16 * 2)
            pool.wait_ge(cleared, 1)

            def fix(it, n):
                m = it * HPT + n
                i, cs = n % 2, n % HPT
                pool.wait_ge(sheared[cs], dma_at(2 * (m // HPT + 1)))
                tables = ((CS[cs], genC[i], 0), (PS[cs], genP[i], S - 1))
                for k, (dst, src, c0) in enumerate(tables):
                    if k == 0:
                        pool.wait_ge(fixed, at(m))
                    r = slice(1, TT) if k == 0 else slice(0, TT - 1)
                    nc.gpsimd.tensor_tensor(tri_val[:, k, :, :],
                                            tri[:, k, :].unsqueeze(1).to_broadcast([P, TT - 1, P]),
                                            src[:, r, c0:c0 + 1].to_broadcast([P, TT - 1, P]),
                                            ALU.mult).then_inc(tri_made, 1)
                for k, (dst, src, c0) in enumerate(tables):
                    for r in ((2, 3) if k == 0 else (0, 1)):
                        lo, hi = (0, (r - 1) * P) if k == 0 else ((r + 2) * P, T)
                        nc.gpsimd.tensor_scalar(dst[:, col(r, lo):col(r, hi)], ones[:, 0:hi - lo],
                                                src[:, r, c0:c0 + 1], None, ALU.mult)
                pool.wait_ge(tri_made, at(2 * m + 2))
                for k, (dst, src, c0) in enumerate(tables):
                    b = dst[:, :]
                    o = bass.AP(b.tensor, b.offset + (col(1, 0) if k == 0 else col(0, P)),
                                [list(b.ap[0]), [T + P, TT - 1], [1, P]])
                    last = nc.gpsimd.tensor_tensor(o, o, tri_val[:, k, :, :], ALU.add)
                last.then_inc(fixed, 1)

            for n in range(2):
                fix(0, n)
            with pool.Fori(0, TURNS) as it:
                for n in range(HPT):
                    fix(it, n + 2)

        @block.scalar
        def _(act):
            def p_copy(it, n, half):
                m = it * HPT + n
                act.wait_ge(p_made, at(2 * m + half + 1))
                act.wait_ge(fixed, at(m - 1))
                nc.scalar.activation(genP[n % 2][:, 2 * half:2 * half + 2, :],
                                     b_P[:, :].rearrange("p (a s) -> p a s", a=2), ACT.Copy).then_inc(p_out, 1)

            for n in range(2):
                for half in range(2):
                    p_copy(0, n, half)
            with act.Fori(0, TURNS) as it:
                for k, t, quarter, tr, use, head in steps():
                    if t is not None:
                        n, qb = t // TT, t % TT
                        act.wait_ge(biased, at(it * TILES + t + 1))
                        act.wait_ge(turned, at(it * TILES + t - 1))
                        act.wait_ge(headed, at(it * HPT + n - 1))
                        nc.scalar.activation(probs[t % 2][:, :], scores[t % 2][:, :], ACT.Exp,
                                             bias=negmax[:, qb:qb + 1], scale=-1.0,
                                             accum_out=sums[n % 2][:, qb:qb + 1]).then_inc(exped, 1)
                    if quarter is not None:
                        p_copy(it, t // TT + 2, quarter)
                    if tr is not None and tr % TT != TT - 1:
                        act.wait_ge(turned, at(it * TILES + tr + 1))
                        act.wait_ge(summed, at(it * TILES + tr - 1))
                        nc.scalar.activation(probsT[tr % 2][:, :, :], b_T[tr % 2][:, :]
                                             .rearrange("p (k q) -> p k q", q=P), ACT.Copy).then_inc(copiedA, 1)

        @block.vector
        def _(dve):
            def c_copy(it, n, half):
                m = it * HPT + n
                dve.wait_ge(c_made, at(2 * m + half + 1))
                dve.wait_ge(fixed, at(m - 1))
                nc.vector.tensor_copy(genC[n % 2][:, 2 * half:2 * half + 2, :],
                                      b_C[:, :].rearrange("p (a s) -> p a s", a=2)).then_inc(c_out, 1)

            dve.wait_ge(cleared, 1)
            for n in range(2):
                for half in range(2):
                    c_copy(0, n, half)
            with dve.Fori(0, TURNS) as it:
                for k, t, quarter, tr, use, head in steps():
                    if t is not None:
                        n, qb = t // TT, t % TT
                        dve.wait_ge(scored, at(it * TILES + t + 1))
                        dve.wait_ge(exped, at(it * TILES + t - 1))
                        dve.sem_inc(settled, 1)
                        nc.vector.tensor_tensor_reduce(
                            out=scores[t % 2][:, :], in0=b_S[t % 2][:, :], in1=CS[n][:, col(qb, 0):col(qb, T)],
                            scale=-SCALE, scalar=BIG, op0=ALU.add, op1=ALU.min,
                            accum_out=negmax[:, qb:qb + 1]).then_inc(biased, 1)
                    if quarter is not None:
                        c_copy(it, t // TT + 2, quarter)
                    if tr is not None and tr % TT == TT - 1:
                        dve.wait_ge(turned, at(it * TILES + tr + 1))
                        dve.wait_ge(summed, at(it * TILES + tr - 1))
                        nc.vector.tensor_copy(probsT[tr % 2][:, :, :], b_T[tr % 2][:, :]
                                              .rearrange("p (k q) -> p k q", q=P)).then_inc(copiedV, 1)
                    if head is not None:
                        dve.wait_ge(exped, at(it * TILES + TT * head + TT))
                        dve.wait_ge(headed, at(it * HPT + head))
                        nc.vector.reciprocal(inv[:, :], sums[head % 2][:, :]).then_inc(inverted, 1)
                        dve.wait_ge(inverted, at(it * HPT + head + 1))
                        dve.wait_ge(summed, at(it * TILES + TT * head + TT))
                        dve.wait_ge(ctx_out, dma_at(it))
                        nc.vector.tensor_tensor(cx[:, :, head * DK:(head + 1) * DK],
                                                b_X[head % 2][:, 0:TT * DK].rearrange("p (t e) -> p t e", e=DK),
                                                inv[:, :].unsqueeze(2).to_broadcast([P, TT, DK]),
                                                ALU.mult).then_inc(headed, 1)

        @block.tensor
        def _(pe):
            def generate(it, n, half):
                m = it * HPT + n
                u, rows = gen_of(n)
                if half == 0:
                    pe.wait_ge(stack_in[u], dma_at(STACK * (m // HPT + 1)))
                for bank, made, out, stack, k in ((b_C, c_made, c_out, stQ, 0), (b_P, p_made, p_out, stK, 1)):
                    pe.wait_ge(out, at(2 * m + half))
                    for a in range(2):
                        blk = 2 * half + a
                        mm = nc.tensor.matmul(bank[:, a * S:(a + 1) * S], stack[u][rows, blk * P:(blk + 1) * P],
                                              tab[u][rows, k, :], start=True, stop=True)
                    mm.then_inc(made, 1)

            pe.wait_ge(consts, 16 * 6)
            for n in range(2):
                for half in range(2):
                    generate(0, n, half)
            with pe.Fori(0, TURNS) as it:
                for k, t, quarter, tr, use, head in steps():
                    if t is not None:
                        n, qb = t // TT, t % TT
                        u, rows = gen_of(n)
                        if qb == 0:
                            pe.wait_ge(fixed, at(it * HPT + n + 1))
                        pe.wait_ge(biased, at(it * TILES + t - 1))
                        blocks = [kb for kb in range(TT) if kb <= qb + 1]
                        nc.tensor.matmul(b_S[t % 2][:, :], stQ[u][rows, qb * P:(qb + 1) * P], stK[u][rows, :],
                                         start=True, stop=True)
                        for kb in blocks:
                            c = col(kb, qb * P)
                            mm = nc.tensor.matmul(b_S[t % 2][:, kb * P:(kb + 1) * P], PS[n][:, c:c + P],
                                                  ident[:, :], start=False, stop=True,
                                                  skip_group_check=True)
                        mm.then_inc(scored, 1)
                    if quarter is not None:
                        generate(it, t // TT + 2, quarter)
                    if tr is not None:
                        pe.wait_ge(exped, at(it * TILES + tr + 1))
                        if tr % TT == 1:
                            pe.wait_ge(copiedV, at(it * HPT + tr // TT))
                        else:
                            pe.wait_ge(copiedA, at(it * 3 * HPT + tr // TT * 3 + max(tr % TT - 1, 0)))
                        for kb in range(TT):
                            mm = nc.tensor.transpose(b_T[tr % 2][:, kb * P:(kb + 1) * P],
                                                     probs[tr % 2][:, kb * P:(kb + 1) * P], ident[:, :])
                        mm.then_inc(turned, 1)
                    if use is not None:
                        n, qb = use // TT, use % TT
                        if qb == TT - 1:
                            pe.wait_ge(copiedV, at(it * HPT + n + 1))
                        else:
                            pe.wait_ge(copiedA, at(it * 3 * HPT + 3 * n + qb + 1))
                        if qb == 0:
                            pe.wait_ge(headed, at(it * HPT + n - 1))
                            pe.wait_ge(val_in[n // 2], dma_at(it + 1))
                        for kb in range(TT):
                            mm = nc.tensor.matmul(b_X[n % 2][:, qb * DK:(qb + 1) * DK], probsT[use % 2][:, kb, :],
                                                  val[n // 2][:, kb, DK * (n % 2):DK * (n % 2) + DK],
                                                  start=kb == 0, stop=kb == TT - 1)
                        mm.then_inc(summed, 1)


def build_post(nc, d):
    with ExitStack() as ctx:
        sb, ps, sem = alloc(nc, ctx)
        ident = sb("po_ident", [P, P])
        wo = sb("po_wo", [P, DC, D])
        wo_hi = sb("po_wohi", [P, DC, D], F32R)
        wo_lo = sb("po_wolo", [P, DC, D], F32R)
        bo = sb("po_bo", [P, D])
        wr = sb("po_wr", [P, DC, E])
        br = sb("po_br", [P, E])
        mod = sb("po_mod", [P, B * 6 * DC])
        power = sb("po_power", [P, TT])
        ct = [sb(f"po_ctx{u}", [P, TT, D]) for u in range(2)]
        xt = [sb(f"po_xt{u}", [P, TT, D]) for u in range(2)]
        ga = [sb(f"po_ga{u}", [P, D]) for u in range(2)]
        mb = sb("po_mb", [P, 6, DC])
        c_hi = sb("po_chi", [P, DC, T], F32R)
        c_lo = sb("po_clo", [P, DC, T], F32R)
        bias = sb("po_bias", [P, D])
        base = sb("po_base", [P, TT, D])
        att = sb("po_att", [P, TT, D])
        x1 = sb("po_x1", [P, TT, D])
        st = sb("po_st", [P, TT, 6])
        mv = sb("po_mv", [P, TT, 2])
        var = sb("po_var", [P, TT])
        rstd = sb("po_rstd", [P, TT])
        hn = sb("po_hn", [P, TT, D])
        hT = sb("po_hT", [P, DC, T])
        logits = sb("po_logits", [P, TT, E])
        ex = sb("po_ex", [P, TT, E])
        den = sb("po_den", [P, TT, E])
        aff = sb("po_aff", [P, TT, E])
        top = sb("po_top", [P, TT, TOPK])
        rest = sb("po_rest", [P, TT, E])
        sel = sb("po_sel", [P, TT, E])
        total = sb("po_total", [P, TT])
        safe = sb("po_safe", [P, TT])
        inv = sb("po_inv", [P, TT])
        wts = sb("po_wts", [P, TT, P])
        wT = sb("po_wT", [EA, T])
        p_c = [ps(f"po_pc{c}") for c in range(DC)]
        p_a = [ps(f"po_pa{i}") for i in range(2)]
        p_h = [ps(f"po_ph{c}") for c in range(DC)]
        p_l, p_w = ps("po_pl"), ps("po_pw")
        loaded, wsplit = sem("po_loaded"), sem("po_wsplit")
        power_set, wts_set = sem("po_power_set"), sem("po_wts_set")
        settled = sem("po_settled")
        ctx_in = [sem("po_ctx_in0"), sem("po_ctx_in1")]
        x_in = [sem("po_x_in0"), sem("po_x_in1")]
        turned, rounded, split = sem("po_turned"), sem("po_rounded"), sem("po_split")
        based, multiplied, added = sem("po_based"), sem("po_multiplied"), sem("po_added")
        scaled = sem("po_scaled")
        stats, powered, normed = sem("po_stats"), sem("po_powered"), sem("po_normed")
        h_turned, modulated = sem("po_h_turned"), sem("po_modulated")
        scored, biased, exped = sem("po_scored"), sem("po_biased"), sem("po_exped")
        routed = sem("po_routed")
        w_turned, w_out = sem("po_w_turned"), sem("po_w_out")
        x1_stored, h_stored, w_stored = sem("po_x1_stored"), sem("po_h_stored"), sem("po_w_stored")
        STATS = 2 * TT + 2
        ROUTED = 2 + 2 * TT + 5
        LOADS = 9
        block = ctx.enter_context(nc.Block())

        @block.sync
        def _(sp):
            credit(sp, [turned, rounded, split, based, multiplied, added, scaled, stats, powered, normed,
                        h_turned, modulated, scored, biased, exped, routed, w_turned, w_out],
                   [x1_stored, h_stored, w_stored])

            def load_ctx(b, u):
                sp.dma_start(ct[u][:, :, :], d["ctxd"][bass.ds(b, 1)].squeeze(0)).then_inc(ctx_in[u], 16)

            def load_x(b, u):
                sp.dma_start(xt[u][:, :, :], d["x"][bass.ds(b, 1)].squeeze(0)
                             .rearrange("(t p) n -> p t n", p=P)).then_inc(x_in[u], 16)
                sp.dma_start(ga[u][:, :], d["modrow"][bass.ds(b, 1)].squeeze(0)[2 * D:3 * D]
                             .partition_broadcast(P)).then_inc(x_in[u], 16)

            for u in range(2):
                load_ctx(u, u)
                load_x(u, u)
            sp.dma_start(ident[:, :], d["ident"]).then_inc(loaded, 16)
            sp.dma_start(wo[:, :, :], d["wo"].rearrange("(c p) n -> p c n", p=P)).then_inc(loaded, 16)
            sp.dma_start(bo[:, :], d["bo"].partition_broadcast(P)).then_inc(loaded, 16)
            sp.dma_start(wr[:, :, :], d["wr"].rearrange("(c p) n -> p c n", p=P)).then_inc(loaded, 16)
            sp.dma_start(br[:, :], d["br"].partition_broadcast(P)).then_inc(loaded, 16)
            sp.dma_start(mod[:, :], d["modcol"].rearrange("p b k c -> p (b k c)")).then_inc(loaded, 16)
            with sp.Fori(0, B // 2) as bb:
                for u in range(2):
                    b = bb * 2 + u
                    sp.wait_ge(turned, at(b + 1))
                    load_ctx((b + 2) % B, u)
                    sp.wait_ge(based, at(2 * b + 2))
                    sp.wait_ge(scaled, at(2 * b + 2))
                    load_x((b + 2) % B, u)
                    sp.wait_ge(added, at(2 * b + 2))
                    sp.dma_start(d["x1"][bass.ds(b, 1)].squeeze(0), x1[:, :, :]).then_inc(x1_stored, 16)
                    sp.wait_ge(modulated, at(DC * b + DC))
                    sp.dma_start(d["h2T"][bass.ds(b, 1)].squeeze(0), hT[:, :, :]).then_inc(h_stored, 16)
                    sp.wait_ge(w_out, at(b + 1))
                    sp.dma_start(d["wT"][:, bass.ds(b * T, T)], wT[:, :]).then_inc(w_stored, 16)
            for s in (x1_stored, h_stored, w_stored):
                sp.wait_ge(s, dma_at(B))
            for u in range(2):
                sp.wait_ge(ctx_in[u], 16 * (B // 2 + 1))
                sp.wait_ge(x_in[u], 16 * 2 * (B // 2 + 1))

        @block.gpsimd
        def _(pool):
            nc.gpsimd.memset(power[:, :], -0.5).then_inc(power_set, 1)
            pool.wait_ge(power_set, 1)
            pool.wait_ge(loaded, 16 * 6)
            with pool.Fori(0, B // 2) as bb:
                for u in range(2):
                    b = bb * 2 + u
                    pool.wait_ge(x_in[u], bb * 32 + 32)
                    nc.gpsimd.tensor_tensor(bias[:, :], bo[:, :], ga[u][:, :], ALU.mult).then_inc(based, 1)
                    pool.wait_ge(based, at(2 * b + 1))
                    pool.wait_ge(added, at(2 * b))
                    nc.gpsimd.tensor_tensor(base[:, :, :], xt[u][:, :, :],
                                            bias[:, :].unsqueeze(1).to_broadcast([P, TT, D]),
                                            ALU.add).then_inc(based, 1)
                    pool.wait_ge(stats, at(b * STATS + STATS))
                    pool.wait_ge(normed, at(b * TT))
                    nc.gpsimd.tensor_tensor(rstd[:, :], var[:, :], power[:, :], ALU.pow).then_inc(powered, 1)

        @block.scalar
        def _(act):
            with act.Fori(0, B) as b:
                act.wait_ge(turned, at(b + 1))
                act.wait_ge(multiplied, at(b * 2))
                for c in range(DC):
                    nc.scalar.activation(c_hi[:, c, :], p_c[c][:, :], ACT.Copy).then_inc(rounded, 1)
                act.wait_ge(h_turned, at(b + 1))
                act.wait_ge(scored, at(b))
                act.wait_ge(h_stored, dma_at(b))
                for c in range(DC):
                    nc.scalar.activation(hT[:, c, :], p_h[c][:, :], ACT.Identity, scale=mb[:, 4, c:c + 1],
                                         bias=mb[:, 3, c:c + 1]).then_inc(modulated, 1)
                act.wait_ge(biased, at(b + 1))
                act.wait_ge(routed, at(b * ROUTED))
                nc.scalar.activation(ex[:, :, :], logits[:, :, :], ACT.Exp, scale=-1.0).then_inc(exped, 1)
                act.wait_ge(w_turned, at(b + 1))
                act.wait_ge(w_stored, dma_at(b))
                nc.scalar.activation(wT[:, :], p_w[0:EA, :], ACT.Copy).then_inc(w_out, 1)

        @block.vector
        def _(dve):
            nc.vector.memset(wts[:, :, :], 1.0).then_inc(wts_set, 1)
            dve.wait_ge(loaded, 16 * 6)
            nc.vector.tensor_copy(wo_hi[:, :, :], wo[:, :, :]).then_inc(wsplit, 1)
            dve.wait_ge(wsplit, 1)
            dve.wait_ge(wts_set, 1)
            nc.vector.tensor_tensor(wo_lo[:, :, :], wo[:, :, :], wo_hi[:, :, :].bitcast(F32),
                                    ALU.subtract).then_inc(wsplit, 1)
            with dve.Fori(0, B // 2) as bb:
                for u in range(2):
                    b = bb * 2 + u
                    dve.wait_ge(multiplied, at(b * 2))
                    for c in range(DC):
                        dve.wait_ge(rounded, at(b * DC + c + 1))
                        nc.vector.tensor_tensor(c_lo[:, c, :], p_c[c][:, :], c_hi[:, c, :].bitcast(F32),
                                                ALU.subtract).then_inc(split, 1)
                    for i in range(2):
                        two = slice(2 * i, 2 * i + 2)
                        dve.wait_ge(multiplied, at(2 * b + i + 1))
                        dve.wait_ge(added, at(2 * b))
                        nc.vector.tensor_tensor(att[:, two, :], p_a[i][:, :].rearrange("p (t n) -> p t n", n=D),
                                                ga[u][:, :].unsqueeze(1).to_broadcast([P, 2, D]),
                                                ALU.mult).then_inc(scaled, 1)
                    dve.wait_ge(based, at(2 * b + 2))
                    dve.wait_ge(x1_stored, dma_at(b))
                    dve.wait_ge(normed, at(b * TT))
                    for i in range(2):
                        two = slice(2 * i, 2 * i + 2)
                        dve.wait_ge(scaled, at(2 * b + i + 1))
                        nc.vector.tensor_tensor(x1[:, two, :], att[:, two, :], base[:, two, :],
                                                ALU.add).then_inc(added, 1)
                    for t in range(TT):
                        if t % 2 == 0:
                            dve.wait_ge(added, at(2 * b + t // 2 + 1))
                        nc.vector.bn_stats(st[:, t, :], x1[:, t, :]).then_inc(stats, 1)
                    dve.wait_ge(modulated, at(b * DC))
                    dve.wait_ge(stats, at(b * STATS + TT))
                    nc.vector.tensor_copy(mb[:, :, :], mod[:, bass.ds(b * (6 * DC), 6 * DC)]
                                          .rearrange("p (k c) -> p k c", c=DC)).then_inc(stats, 1)
                    for t in range(TT):
                        nc.vector.bn_aggr(mv[:, t, :], st[:, t, :]).then_inc(stats, 1)
                    dve.wait_ge(stats, at(b * STATS + 1 + 2 * TT))
                    nc.vector.tensor_scalar_add(var[:, :], mv[:, :, 1], EPS).then_inc(stats, 1)
                    dve.wait_ge(powered, at(b + 1))
                    dve.wait_ge(h_turned, at(b))
                    for t in range(TT):
                        nc.vector.tensor_scalar(hn[:, t, :], x1[:, t, :], mv[:, t, 0:1], rstd[:, t:t + 1],
                                                ALU.subtract, ALU.mult).then_inc(normed, 1)
                    dve.wait_ge(scored, at(b + 1))
                    dve.wait_ge(exped, at(b))
                    nc.vector.tensor_tensor(logits[:, :, :], p_l[:, 0:TT * E].rearrange("p (t e) -> p t e", e=E),
                                            br[:, :].unsqueeze(1).to_broadcast([P, TT, E]),
                                            ALU.add).then_inc(biased, 1)

                    def ready(n):
                        dve.wait_ge(routed, at(b * ROUTED + n))

                    dve.wait_ge(exped, at(b + 1))
                    nc.vector.tensor_scalar_add(den[:, :, :], ex[:, :, :], 1.0).then_inc(routed, 1)
                    ready(1)
                    nc.vector.reciprocal(aff[:, :, :], den[:, :, :]).then_inc(routed, 1)
                    ready(2)
                    dve.sem_inc(settled, 1)
                    for t in range(TT):
                        nc.vector.max(top[:, t, :], aff[:, t, :]).then_inc(routed, 1)
                    for t in range(TT):
                        ready(2 + t + 1)
                        dve.sem_inc(settled, 1)
                        nc.vector.match_replace(rest[:, t, :], top[:, t, :], aff[:, t, :], 0.0).then_inc(routed, 1)
                    ready(2 + 2 * TT)
                    nc.vector.tensor_tensor(sel[:, :, :], aff[:, :, :], rest[:, :, :], ALU.subtract)\
                        .then_inc(routed, 1)
                    nc.vector.tensor_reduce(total[:, :], top[:, :, :], mybir.AxisListType.X, ALU.add)\
                        .then_inc(routed, 1)
                    ready(2 + 2 * TT + 2)
                    nc.vector.tensor_scalar_add(safe[:, :], total[:, :], 1e-9).then_inc(routed, 1)
                    ready(2 + 2 * TT + 3)
                    nc.vector.reciprocal(inv[:, :], safe[:, :]).then_inc(routed, 1)
                    ready(2 + 2 * TT + 4)
                    dve.wait_ge(w_turned, at(b))
                    nc.vector.tensor_tensor(wts[:, :, 0:E], sel[:, :, :],
                                            inv[:, :].unsqueeze(2).to_broadcast([P, TT, E]),
                                            ALU.mult).then_inc(routed, 1)

        @block.tensor
        def _(pe):
            pe.wait_ge(loaded, 16 * 6)
            pe.wait_ge(wsplit, 2)
            with pe.Fori(0, B // 2) as bb:
                for u in range(2):
                    b = bb * 2 + u
                    pe.wait_ge(ctx_in[u], bb * 16 + 16)
                    pe.wait_ge(split, at(b * DC))
                    for t in range(TT):
                        for c in range(DC):
                            m = nc.tensor.transpose(p_c[c][:, t * P:(t + 1) * P], ct[u][:, t, c * P:(c + 1) * P],
                                                    ident[:, :])
                    m.then_inc(turned, 1)
                    pe.wait_ge(rounded, at(b * DC + DC))
                    pe.wait_ge(split, at(b * DC + DC))
                    for i in range(2):
                        pe.wait_ge(scaled, at(2 * b))
                        for t in (2 * i, 2 * i + 1):
                            prods = [(h, w, c) for h, w in ((c_hi, wo_hi), (c_hi, wo_lo), (c_lo, wo_hi))
                                     for c in range(DC)]
                            for n, (h, w, c) in enumerate(prods):
                                m = nc.tensor.matmul(p_a[i][:, (t % 2) * D:(t % 2) * D + D],
                                                     h[:, c, t * P:(t + 1) * P], w[:, c, :],
                                                     start=n == 0, stop=n == len(prods) - 1)
                        m.then_inc(multiplied, 1)
                    pe.wait_ge(modulated, at(b * DC))
                    for t in range(TT):
                        pe.wait_ge(normed, at(b * TT + t + 1))
                        for c in range(DC):
                            m = nc.tensor.transpose(p_h[c][:, t * P:(t + 1) * P], hn[:, t, c * P:(c + 1) * P],
                                                    ident[:, :])
                    m.then_inc(h_turned, 1)
                    pe.wait_ge(modulated, at(b * DC + DC))
                    pe.wait_ge(biased, at(b))
                    for t in range(TT):
                        for c in range(DC):
                            m = nc.tensor.matmul(p_l[:, t * E:(t + 1) * E], hT[:, c, t * P:(t + 1) * P],
                                                 wr[:, c, :], start=c == 0, stop=c == DC - 1)
                    m.then_inc(scored, 1)
                    pe.wait_ge(routed, at(b * ROUTED + ROUTED))
                    pe.wait_ge(w_out, at(b))
                    for t in range(TT):
                        m = nc.tensor.transpose(p_w[:, t * P:(t + 1) * P], wts[:, t, :], ident[:, :])
                    m.then_inc(w_turned, 1)


def build_experts(nc, d):
    with ExitStack() as ctx:
        sb, ps, sem = alloc(nc, ctx)
        HALVES = BLK // T
        EPT = 3
        TURNS = EA // EPT
        UNITS = EPT * HALVES
        PAR = HALVES * DC
        bd = sb("ex_bd", [EA, D])
        h_raw = sb("ex_hraw", [P, PAR, T])
        h_hi = sb("ex_hhi", [P, 2 * PAR, T], F32R)
        h_lo = sb("ex_hlo", [P, 2 * PAR, T], F32R)
        raw = [sb(f"ex_raw{j}", [P, WCOLS + 2]) for j in range(EPT)]
        w_hi = [sb(f"ex_whi{j}", [P, WCOLS], F32R) for j in range(EPT)]
        w_lo = [sb(f"ex_wlo{j}", [P, WCOLS], F32R) for j in range(EPT)]
        share = [sb(f"ex_share{j}", [P, BLK]) for j in range(EPT)]
        silu = [sb(f"ex_silu{i}", [P, T]) for i in range(2)]
        gated = [sb(f"ex_gated{i}", [P, T]) for i in range(2)]
        hid = [sb(f"ex_hid{i}", [P, T]) for i in range(2)]
        hid_hi = [sb(f"ex_hidhi{i}", [P, T], F32R) for i in range(2)]
        hid_lo = [sb(f"ex_hidlo{i}", [P, T], F32R) for i in range(2)]
        wT = sb("ex_wT", [EA, BLK])
        x1 = sb("ex_x1", [P, HALVES * TT, D])
        gb = sb("ex_gb", [P, HALVES, D])
        scaled = sb("ex_scaled", [P, HALVES * TT, D])
        out = sb("ex_out", [P, HALVES * TT, D])
        p_o = [ps(f"ex_po{i}") for i in range(4)]
        p_g = [ps(f"ex_pg{i}") for i in range(2)]
        p_u = [ps(f"ex_pu{i}") for i in range(2)]
        bd_in, h_in, wT_in, res_in = sem("ex_bd_in"), sem("ex_h_in"), sem("ex_wT_in"), sem("ex_res_in")
        w_in = [sem(f"ex_w_in{j}") for j in range(EPT)]
        w_rounded, w_split, h_split = sem("ex_w_rounded"), sem("ex_w_split"), sem("ex_h_split")
        gate_made, up_made, started, summed = (sem("ex_gate_made"), sem("ex_up_made"), sem("ex_started"),
                                               sem("ex_summed"))
        silued, steps, rounded, split = sem("ex_silued"), sem("ex_steps"), sem("ex_rounded"), sem("ex_split")
        scale_done, out_ready, out_stored = sem("ex_scale_done"), sem("ex_out_ready"), sem("ex_out_stored")
        block = ctx.enter_context(nc.Block())

        @block.sync
        def _(sp):
            credit(sp, [w_rounded, w_split, h_split, gate_made, up_made, started, summed, silued, steps, rounded,
                        split, scale_done, out_ready], w_in + [h_in, wT_in, res_in, out_stored])
            sp.dma_start(bd[:, :], d["bd"]).then_inc(bd_in, 16)

            def load_weights(x, j):
                e, blk = x % EA, x // EA % NBLK
                sp.dma_start(raw[j][:, :], d["wexp"][bass.ds(e, 1)].squeeze(0)).then_inc(w_in[j], 16)
                sp.dma_start(share[j][:, :], d["wT"][bass.ds(e, 1)].squeeze(0)[bass.ds(blk * BLK, BLK)]
                             .partition_broadcast(P)).then_inc(w_in[j], 16)

            def load_hidden(blk):
                sp.dma_start(h_raw[:, :, :].rearrange("p (h c) t -> p h (c t)", c=DC),
                             d["h2T"][bass.ds(blk * HALVES, HALVES)].rearrange("h p c t -> p h (c t)"))\
                    .then_inc(h_in, 16)

            def load_wT(blk):
                sp.dma_start(wT[:, :], d["wT"][:, bass.ds(blk * BLK, BLK)]).then_inc(wT_in, 16)

            load_hidden(0)
            for j in range(EPT):
                load_weights(j, j)
            load_wT(0)
            with sp.Fori(0, NBLK) as blk:
                sp.wait_ge(h_split, at(2 * blk + 2))
                load_hidden((blk + 1) % NBLK)
                sp.wait_ge(started, at(4 * blk + 4))
                load_wT((blk + 1) % NBLK)
                sp.wait_ge(out_ready, at(4 * blk))
                sp.dma_start(x1[:, :, :].rearrange("p (h t) n -> p h (t n)", t=TT),
                             d["x1"][bass.ds(blk * HALVES, HALVES)].rearrange("h p t n -> p h (t n)"))\
                    .then_inc(res_in, 16)
                for h in range(HALVES):
                    sp.dma_start(gb[:, h, :], d["modrow"][bass.ds(blk * HALVES + h, 1)].squeeze(0)
                                 [5 * D:6 * D].partition_broadcast(P)).then_inc(res_in, 16)
                with sp.Fori(0, TURNS) as turn:
                    for j in range(EPT):
                        x = blk * EA + turn * EPT + j
                        sp.wait_ge(steps, at(4 * x + 4))
                        load_weights(x + EPT, j)
                for i in range(4):
                    sp.wait_ge(out_ready, at(4 * blk + i + 1))
                    sp.dma_start(d["out"][bass.ds(blk * HALVES + i // 2, 1)].squeeze(0)
                                 .rearrange("(t p) n -> p t n", p=P)[:, 2 * (i % 2):2 * (i % 2) + 2, :],
                                 out[:, 2 * i:2 * i + 2, :]).then_inc(out_stored, 16)
            sp.wait_ge(out_stored, dma_at(4 * NBLK))
            sp.wait_ge(h_in, dma_at(NBLK + 1))
            sp.wait_ge(wT_in, dma_at(NBLK + 1))
            for j in range(EPT):
                sp.wait_ge(w_in[j], dma_at(2 * (NBLK * TURNS + 1)))

        @block.gpsimd
        def _(pool):
            def split_hidden(blk):
                s = bass.ds(blk % 2 * PAR, PAR)
                pool.wait_ge(h_in, dma_at(blk + 1))
                nc.gpsimd.tensor_copy(h_hi[:, s, :], h_raw[:, :, :]).then_inc(h_split, 1)
                pool.wait_ge(h_split, at(2 * blk + 1))
                nc.gpsimd.tensor_tensor(h_lo[:, s, :], h_raw[:, :, :], h_hi[:, s, :].bitcast(F32),
                                        ALU.subtract).then_inc(h_split, 1)

            def split_weights(x, j):
                pool.wait_ge(w_rounded, at(x + 1))
                nc.gpsimd.tensor_tensor(w_lo[j][:, :], raw[j][:, 0:WCOLS], w_hi[j][:, :].bitcast(F32),
                                        ALU.subtract).then_inc(w_split, 1)

            split_hidden(0)
            for j in range(2):
                split_weights(j, j)
            with pool.Fori(0, NBLK) as blk:
                pool.wait_ge(started, at(4 * blk + 4))
                split_hidden(blk + 1)
                with pool.Fori(0, TURNS) as turn:
                    for j in range(EPT):
                        split_weights(blk * EA + turn * EPT + j + 2, (j + 2) % EPT)
                pool.wait_ge(res_in, dma_at(3 * blk + 3))
                pool.wait_ge(out_stored, dma_at(4 * blk))
                for i in range(4):
                    two = slice(2 * i, 2 * i + 2)
                    pool.wait_ge(scale_done, at(4 * blk + i + 1))
                    nc.gpsimd.tensor_tensor(out[:, two, :], scaled[:, two, :], x1[:, two, :],
                                            ALU.add).then_inc(out_ready, 1)

        @block.scalar
        def _(act):
            def round_weights(x, j, turns):
                act.wait_ge(w_in[j], dma_at(2 * turns))
                act.wait_ge(summed, at(2 * x - 4))
                nc.scalar.activation(w_hi[j][:, :], raw[j][:, 0:WCOLS], ACT.Copy).then_inc(w_rounded, 1)

            for j in range(2):
                round_weights(j, j, 1)
            with act.Fori(0, NBLK) as blk:
                with act.Fori(0, TURNS) as turn:
                    for j in range(EPT):
                        x = blk * EA + turn * EPT + j
                        for h in range(HALVES):
                            n = 2 * x + h
                            act.wait_ge(gate_made, at(n + 1))
                            act.wait_ge(steps, at(2 * n - 3))
                            nc.scalar.activation(silu[h][:, :], p_g[h][:, :], ACT.Silu,
                                                 bias=raw[j][:, WCOLS:WCOLS + 1]).then_inc(silued, 1)
                            if h == 0:
                                round_weights(x + 2, (j + 2) % EPT,
                                              blk * TURNS + turn + (1 if j == 0 else 2))
                            act.wait_ge(steps, at(2 * n + 2))
                            act.wait_ge(summed, at(n - 1))
                            nc.scalar.activation(hid_hi[h][:, :], hid[h][:, :], ACT.Copy).then_inc(rounded, 1)

        @block.vector
        def _(dve):
            with dve.Fori(0, NBLK) as blk:
                with dve.Fori(0, TURNS) as turn:
                    for j in range(EPT):
                        x = blk * EA + turn * EPT + j
                        for h in range(HALVES):
                            n = 2 * x + h
                            dve.wait_ge(up_made, at(n + 1))
                            dve.wait_ge(silued, at(n + 1))
                            nc.vector.scalar_tensor_tensor(out=gated[h][:, :], in0=p_u[h][:, :],
                                                           scalar=raw[j][:, WCOLS + 1:WCOLS + 2], in1=silu[h][:, :],
                                                           op0=ALU.add, op1=ALU.mult).then_inc(steps, 1)
                            dve.wait_ge(w_in[j], dma_at(2 * (blk * TURNS + turn + 1)))
                            dve.wait_ge(split, at(n - 1))
                            dve.wait_ge(steps, at(2 * n + 1))
                            nc.vector.tensor_tensor(hid[h][:, :], gated[h][:, :], share[j][:, h * T:(h + 1) * T],
                                                    ALU.mult).then_inc(steps, 1)
                            dve.wait_ge(rounded, at(n + 1))
                            nc.vector.tensor_tensor(hid_lo[h][:, :], hid[h][:, :], hid_hi[h][:, :].bitcast(F32),
                                                    ALU.subtract).then_inc(split, 1)
                dve.wait_ge(res_in, dma_at(3 * blk + 3))
                for i in range(4):
                    two = slice(2 * i, 2 * i + 2)
                    dve.wait_ge(summed, at(2 * EA * blk + 2 * EA))
                    dve.wait_ge(out_ready, at(4 * blk))
                    nc.vector.tensor_tensor(scaled[:, two, :], p_o[i][:, :].rearrange("p (t n) -> p t n", n=D),
                                            gb[:, i // 2, :].unsqueeze(1).to_broadcast([P, 2, D]),
                                            ALU.mult).then_inc(scale_done, 1)

        @block.tensor
        def _(pe):
            def gate_up(n, j, h, blk):
                if h == 0:
                    pe.wait_ge(w_rounded, at(n // 2 + 1))
                    pe.wait_ge(w_split, at(n // 2 + 1))
                    pe.wait_ge(h_split, at(2 * blk + 2))
                for bank, made, c0, free, seen in ((p_g[h], gate_made, 0, silued, at(n - 1)),
                                                   (p_u[h], up_made, DC * I, steps, at(2 * n - 3))):
                    pe.wait_ge(free, seen)
                    prods = [(w, x, c) for w, x in ((w_hi, h_hi), (w_hi, h_lo), (w_lo, h_hi)) for c in range(DC)]
                    for k, (w, x, c) in enumerate(prods):
                        mm = nc.tensor.matmul(bank[:, :], w[j][:, c0 + c * I:c0 + (c + 1) * I],
                                              x[:, bass.ds(blk % 2 * PAR + h * DC + c, 1), :].squeeze(1),
                                              start=k == 0, stop=k == len(prods) - 1)
                    mm.then_inc(made, 1)

            def down(n, j, h):
                pe.wait_ge(rounded, at(n + 1))
                pe.wait_ge(split, at(n + 1))
                for t in range(TT):
                    tile = h * TT + t
                    o = p_o[tile // 2][:, tile % 2 * D:tile % 2 * D + D]
                    s, w0 = slice(t * P, (t + 1) * P), slice(2 * DC * I, WCOLS)
                    for x, w in ((hid_hi, w_hi), (hid_hi, w_lo), (hid_lo, w_hi)):
                        mm = nc.tensor.matmul(o, x[h][:, s], w[j][:, w0], start=False, stop=True,
                                              skip_group_check=True)
                mm.then_inc(summed, 1)

            for h in range(HALVES):
                gate_up(h, 0, h, 0)
            pe.wait_ge(bd_in, 16)
            with pe.Fori(0, NBLK) as blk:
                pe.wait_ge(wT_in, dma_at(blk + 1))
                for i in range(4):
                    pe.wait_ge(scale_done, at(4 * blk - 3 + i))
                    for t in (2 * i, 2 * i + 1):
                        mm = nc.tensor.matmul(p_o[i][:, t % 2 * D:t % 2 * D + D], wT[:, t * P:(t + 1) * P],
                                              bd[:, :], start=t % 2 == 0, stop=True, skip_group_check=True)
                    mm.then_inc(started, 1)
                with pe.Fori(0, TURNS) as turn:
                    for u in range(UNITS):
                        j, h = u // 2, u % 2
                        n = blk * (2 * EA) + turn * UNITS + u
                        down(n, j, h)
                        gate_up(n + 2, (j + 1) % EPT, h,
                                blk if u < UNITS - 2 else (blk * TURNS + turn + 1) // TURNS)


def build(nc, d):
    with ExitStack() as ctx:
        sb = lambda name, shape: ctx.enter_context(nc.sbuf_tensor(name, shape, F32))
        dram = lambda name, shape: nc.dram_tensor(name, shape, F32, kind="Internal").ap()
        d["qkbias"] = sb("qkbias", [P, 4])
        size = P + TT * P * PITCH + P
        d["scrC"] = dram("scrC", (2, size))
        d["scrP"] = dram("scrP", (2, size))
        d["tabs"] = dram("tabs", (PAIRS, P, 2, S))
        d["modrow"] = dram("modrow", (B, 6 * D))
        d["modcol"] = dram("modcol", (P, B, 6, DC))
        d["stackQ"] = dram("stackQ", (B * H, 3, DK, T))
        d["stackK"] = dram("stackK", (B * H, 3, DK, T))
        d["headpad"] = dram("headpad", (DK, T))
        d["vals"] = dram("vals", (B, P, TT, D))
        d["ctxd"] = dram("ctxd", (B, P, TT, D))
        d["x1"] = dram("x1", (B, P, TT, D))
        d["h2T"] = dram("h2T", (B, P, DC, T))
        d["wT"] = dram("wT", (EA, B * T))
        build_setup(nc, d)
        build_qkv(nc, d)
        build_attention(nc, d)
        build_post(nc, d)
        build_experts(nc, d)


def laid_out(i):
    import numpy as np
    f = lambda k: np.asarray(i[k])
    a = {}
    a["x"] = f("L0_attn_x")
    for k in ("q", "k", "v", "o"):
        a["w" + k] = f("L0_attn_W" + k).T
    col = lambda v: v.reshape(DC, P).T
    a["bqk"] = np.stack([np.concatenate([col(f("L0_attn_bq")), col(f("L0_attn_bk"))], 1),
                         np.concatenate([col(f("L0_attn_bpq")), col(f("L0_attn_bpk"))], 1)], 2)
    a["bv"], a["bo"] = f("L0_attn_bv"), f("L0_attn_bo")

    def stacked(w):
        out = np.zeros((w.shape[0], H, 4, DK), w.dtype)
        out[:, :, 0:3] = w.reshape(w.shape[0], H, 1, DK)
        return out.reshape(w.shape[0], PAIRS * P)

    a["wpk"], a["wpq"] = stacked(f("L0_attn_Wpk").T), stacked(f("L0_attn_Wpq").T)
    a["wpos"] = np.concatenate([f("L0_attn_Wpq").T, f("L0_attn_Wpk").T], 1)
    a["bpos"] = np.stack([stacked(f(k)[None])[0].reshape(PAIRS, P).T
                          for k in ("L0_attn_bpk", "L0_attn_bpq")], 1)
    a["relT"] = f("L0_attn_rel_emb").T
    a["relTr"] = f("L0_attn_rel_emb")[::-1].T
    a["cT"] = f("L0_c").T
    a["wmod"] = f("L0_wmod")
    a["wr"], a["br"] = f("L0_ffn_Wr"), f("L0_ffn_br")

    def by_expert(routed, shared):
        return np.concatenate([f(routed), f(shared)[None]], 0)

    def rows(w):
        return w.reshape(EA, DC, P, -1).transpose(0, 2, 1, 3).reshape(EA, P, -1)

    a["wexp"] = np.concatenate([rows(by_expert("L0_ffn_Wg", "L0_ffn_Wg_s")), rows(by_expert("L0_ffn_Wu", "L0_ffn_Wu_s")),
                                by_expert("L0_ffn_Wd", "L0_ffn_Wd_s"),
                                by_expert("L0_ffn_bg", "L0_ffn_bg_s")[:, :, None],
                                by_expert("L0_ffn_bu", "L0_ffn_bu_s")[:, :, None]], 2)
    a["bd"] = by_expert("L0_ffn_bd", "L0_ffn_bd_s")
    a["ident"] = np.eye(P, dtype=np.float32)
    part = (np.arange(P) % 64) // DK
    row = np.arange(P) % 64
    hi1 = (part <= 1) | (row == 3 * DK)
    lo1 = (part == 2) | (row == 3 * DK + 1)
    hi2, lo2 = (part == 0) | (part == 2), part == 1
    mask = np.zeros((P, 4), np.float32)
    for k, (hi, lo) in enumerate(((hi1, lo1), (hi2, lo2))):
        mask[hi, 2 * k], mask[lo, 2 * k], mask[lo, 2 * k + 1] = 1.0, -1.0, 1.0
    a["rowmask"] = mask
    fsel = np.zeros((P, P), np.float32)
    for j in range(2):
        fsel[64 * j:64 * j + DK, 64 * j + 3 * DK:64 * j + 3 * DK + 2] = 1.0
    a["fsel"] = fsel
    a["pad"] = np.zeros((DK, T), np.float32)
    a["pad"][0:2] = 1.0
    r = np.arange(P)
    a["tri"] = np.stack([(r[None, :] < r[:, None]), (r[None, :] > r[:, None])], 1).astype(np.float32)
    return {k: np.ascontiguousarray(v) for k, v in a.items()}


def kernel(**inputs):
    import concourse.bacc as bacc
    from concourse.bass_utils import run_bass_kernel_spmd

    nc = bacc.Bacc("TRN2", target_bir_lowering=False, num_devices=1)
    arrays = laid_out(inputs)
    d = {k: nc.dram_tensor("in_" + k, v.shape, F32, kind="ExternalInput").ap() for k, v in arrays.items()}
    d["out"] = nc.dram_tensor("out", (B, T, D), F32, kind="ExternalOutput").ap()
    build(nc, d)
    r = run_bass_kernel_spmd(nc, [{"in_" + k: v for k, v in arrays.items()}], core_ids=[0])
    return r.results[0]["out"]
```

```python
from contextlib import ExitStack

import concourse.bass as bass
from concourse import mybir

F32 = mybir.dt.float32
F32R = mybir.dt.float32r
ALU = mybir.AluOpType
ACT = mybir.ActivationFunctionType

P = 128
B, T, D = 16, 512, 256
DC = D // P
TT = T // P
H, DK = 16, 16
DKS = DK + 1
PAIRS = H // 2
SPAN = 128
S = 2 * SPAN
PITCH = S + SPAN
WIN = PITCH
CSW = SPAN + T * TT + SPAN
SCALE = 1.0 / float(DK * 3) ** 0.5
E, I, TOPK = 32, 128, 8
EA = E + 1
WCOLS = 2 * DC * I + D
BLK = 1024
NBLK = B * T // BLK
EPS = 1e-5
BIG = 3.0e38
CREDIT = 16



def at(n):
    return n + CREDIT


def dma_at(n):
    return 16 * (n + CREDIT)


def credit(eng, sems, dma_sems):
    for s in sems:
        eng.sem_inc(s, CREDIT)
    for s in dma_sems:
        eng.sem_inc(s, 16 * CREDIT)


def alloc(nc, ctx):
    def sb(name, shape, dt=F32):
        return ctx.enter_context(nc.sbuf_tensor(name, shape, dt))

    def ps(name, shape=(P, 512)):
        return ctx.enter_context(nc.psum_tensor(name, list(shape), F32))

    def sem(name):
        return ctx.enter_context(nc.semaphore(name))

    return sb, ps, sem


def build_setup(nc, d):
    with ExitStack() as ctx:
        sb, ps, sem = alloc(nc, ctx)
        ident = sb("su_ident", [P, P])
        cT = sb("su_cT", [P, DC, B])
        sig = sb("su_sig", [P, DC, B])
        silu = sb("su_silu", [P, DC, B])
        wmod = sb("su_wmod", [P, DC, 6 * D])
        rows = sb("su_rows", [B, 6 * D])
        sgn = sb("su_sgn", [B, D])
        mag = sb("su_mag", [B, D])
        cols = sb("su_cols", [P, B, 6, DC])
        csgn = sb("su_csgn", [P, B, DC])
        cmag = sb("su_cmag", [P, B, DC])
        rel = sb("su_rel", [P, DC, 2, S])
        wpk = sb("su_wpk", [P, DC, PAIRS * P])
        wpq = sb("su_wpq", [P, DC, PAIRS * P])
        wpos = sb("su_wpos", [P, DC, 2 * D])
        bpos = sb("su_bpos", [P, 2, PAIRS])
        bqk = sb("su_bqk", [P, 4, 2])
        basis = sb("su_basis", [P, 4])
        fsel = sb("su_fsel", [P, P])
        rmask = sb("su_rmask", [P, 4])
        raw = sb("su_raw", [P, 3, S])
        delta = sb("su_delta", [P, 3, S])
        nega = sb("su_nega", [P, 2])
        fl = sb("su_fl", [P, 2, P])
        full = sb("su_full", [P, S])
        part = sb("su_part", [P, 2, S], F32R)
        tab = sb("su_tab", [P, 2, 2, S])
        zero = sb("su_zero", [P, 3072])
        p_a, p_b = ps("su_pa"), ps("su_pb")
        p_t = [ps(f"su_pt{i}") for i in range(4)]
        loaded = sem("su_loaded")
        zeroed, zdone = sem("su_zeroed"), sem("su_zdone")
        exp_done = sem("su_exp")
        step = sem("su_step")
        modp = sem("su_modp")
        tabp = sem("su_tabp")
        biased = sem("su_biased")
        tab_ready, stored, fp = sem("su_tab_ready"), [sem("su_st0"), sem("su_st1")], sem("su_fp")
        mod_made, mod_stored = sem("su_mod_made"), sem("su_mod_stored")
        fsum = sem("su_fsum")
        block = ctx.enter_context(nc.Block())
        marks = {}

        @block.sync
        def _(sp):
            sp.dma_start(cT[:, :, :], d["cT"].rearrange("(c p) b -> p c b", p=P)).then_inc(loaded, 16)
            sp.dma_start(wmod[:, :, :], d["wmod"].rearrange("(c p) n -> p c n", p=P)).then_inc(loaded, 16)
            sp.dma_start(rel[:, :, 0, :], d["relT"].rearrange("(c p) n -> p c n", p=P)).then_inc(loaded, 16)
            sp.dma_start(rel[:, :, 1, :], d["relTr"].rearrange("(c p) n -> p c n", p=P)).then_inc(loaded, 16)
            sp.dma_start(wpk[:, :, :], d["wpk"].rearrange("(c p) n -> p c n", p=P)).then_inc(loaded, 16)
            sp.dma_start(wpq[:, :, :], d["wpq"].rearrange("(c p) n -> p c n", p=P)).then_inc(loaded, 16)
            sp.dma_start(bpos[:, :, :], d["bpos"]).then_inc(loaded, 16)
            sp.dma_start(fsel[:, :], d["fsel"]).then_inc(loaded, 16)
            sp.dma_start(rmask[:, :], d["rowmask"]).then_inc(loaded, 16)
            sp.dma_start(bqk[:, :, :], d["bqk"]).then_inc(loaded, 16)
            sp.dma_start(wpos[:, :, :], d["wpos"].rearrange("(c p) n -> p c n", p=P)).then_inc(loaded, 16)
            sp.dma_start(d["headpad"], d["pad"]).then_inc(zdone, 16)
            sp.wait_ge(zeroed, 1)
            n = 16
            for t in ("scrC", "scrP"):
                for i in range(d[t].shape[0]):
                    size = d[t].shape[1] - 2 * P
                    sp.dma_start(d[t][i, 0:size].rearrange("(p n) -> p n", p=P),
                                 zero[:, 0:size // P]).then_inc(zdone, 16)
                    sp.dma_start(d[t][i, size:size + 2 * P].rearrange("(p n) -> p n", p=P),
                                 zero[:, 0:2]).then_inc(zdone, 16)
                    n += 32
            for g in range(PAIRS):
                sp.wait_ge(tab_ready, g + 1)
                sp.dma_start(d["tabs"][g], tab[:, g % 2, :, :]).then_inc(stored[g % 2], 16)
            sp.wait_ge(zdone, n)
            for s in stored:
                sp.wait_ge(s, 16 * PAIRS // 2)

        @block.gpsimd
        def _(pool):
            nc.gpsimd.memset(zero[:, :], 0.0).then_inc(zeroed, 1)

        @block.scalar
        def _(act):
            act.wait_ge(loaded, 16 * 11)
            nc.scalar.activation(sig[:, :, :], cT[:, :, :], ACT.Exp, scale=-1.0).then_inc(exp_done, 1)
            for g in range(PAIRS):
                act.wait_ge(tabp, g + 1)
                if g:
                    act.wait_ge(fsum, g)
                for i in range(3):
                    kind = 0 if i == 0 else 1
                    a = nc.scalar.activation(raw[:, i, :], p_t[i][:, 0:S], ACT.Identity,
                                             bias=bpos[:, kind, g:g + 1])
                    a.then_inc(biased, 1)
            act.wait_ge(mod_made, 2)
            act.dma_start(d["modrow"], rows[:, :]).then_inc(mod_stored, 16)
            act.dma_start(d["modcol"], cols[:, :, :, :]).then_inc(mod_stored, 16)
            act.wait_ge(mod_stored, 32)

        @block.vector
        def _(dve):
            done = [0]

            def link(ins):
                done[0] += 1
                ins.then_inc(step, 1)
                dve.wait_ge(step, done[0])

            dve.wait_ge(exp_done, 1)
            link(nc.vector.tensor_scalar_add(sig[:, :, :], sig[:, :, :], 1.0))
            link(nc.vector.reciprocal(sig[:, :, :], sig[:, :, :]))
            link(nc.vector.tensor_tensor(silu[:, :, :], sig[:, :, :], cT[:, :, :], ALU.mult))
            marks["silu"] = done[0]
            for n in range(3):
                dve.wait_ge(modp, n + 1)
                link(nc.vector.tensor_copy(rows[:, n * 512:(n + 1) * 512], p_a[0:B, :]))
                marks["row", n] = done[0]
            for k in (2, 5):
                g = rows[:, k * D:(k + 1) * D]
                link(nc.vector.tensor_scalar(sgn[:, :], g, 0.0, 2.0, ALU.is_ge, ALU.mult))
                link(nc.vector.tensor_scalar(mag[:, :], g, -1.0, None, ALU.mult))
                link(nc.vector.tensor_tensor(mag[:, :], g, mag[:, :], ALU.max))
                link(nc.vector.tensor_scalar(mag[:, :], mag[:, :], 0.25, None, ALU.max))
                link(nc.vector.scalar_tensor_tensor(out=g, in0=sgn[:, :], scalar=-1.0, in1=mag[:, :],
                                                    op0=ALU.add, op1=ALU.mult))
            nc.vector.tensor_copy(sgn[:, 0:1], mag[:, 0:1]).then_inc(mod_made, 1)
            dve.wait_ge(modp, 4)
            src = p_b[:, 0:6 * DC * B].rearrange("p (k c b) -> p b k c", k=6, c=DC)
            link(nc.vector.tensor_copy(cols[:, :, :, :], src))
            for k in (1, 4):
                link(nc.vector.tensor_scalar_add(cols[:, :, k, :], cols[:, :, k, :], 1.0))
            g, cs, cm = cols[:, :, 5, :], csgn[:, :, :], cmag[:, :, :]
            link(nc.vector.tensor_scalar(cs, g, 0.0, 2.0, ALU.is_ge, ALU.mult))
            link(nc.vector.tensor_scalar(cm, g, -1.0, None, ALU.mult))
            link(nc.vector.tensor_tensor(cm, g, cm, ALU.max))
            link(nc.vector.tensor_scalar(cm, cm, 0.25, None, ALU.max))
            link(nc.vector.scalar_tensor_tensor(out=g, in0=cs, scalar=-1.0, in1=cm, op0=ALU.add, op1=ALU.mult))
            nc.vector.tensor_copy(mag[:, 0:1], sgn[:, 0:1]).then_inc(mod_made, 1)

            dve.wait_ge(modp, 5)
            dve.wait_ge(loaded, 16 * 11)
            link(nc.vector.tensor_tensor(basis[:, :], p_a[:, 0:4], bqk[:, :, 0], ALU.add))
            link(nc.vector.tensor_tensor(d["qkbias"][:, :], basis[:, :], bqk[:, :, 1], ALU.add))

            for g in range(PAIRS):
                dve.wait_ge(biased, 3 * (g + 1))
                base = [raw[:, 0, S - 1:S], raw[:, 1, S - 1:S], raw[:, 2, 0:1]]
                for i in range(3):
                    link(nc.vector.tensor_scalar(delta[:, i, :], raw[:, i, :], base[i], None, ALU.subtract))
                link(nc.vector.tensor_scalar(nega[:, 0:1], base[1], -1.0, None, ALU.mult))
                link(nc.vector.tensor_scalar(nega[:, 1:2], base[0], -1.0, None, ALU.mult))
                if g == 0:
                    dve.wait_ge(loaded, 16 * 11)
                for i in range(2):
                    link(nc.vector.tensor_scalar(fl[:, i, :], fsel[:, :], nega[:, i:i + 1], None, ALU.mult))
                marks["delta", g] = done[0]
                dve.wait_ge(fp, g + 1)
                link(nc.vector.tensor_tensor(full[:, :], p_t[3][:, 0:S], delta[:, 0, :], ALU.add))
                if g >= 2:
                    dve.wait_ge(stored[g % 2], 16 * (g // 2))
                for i, src in ((0, full[:, :]), (1, delta[:, 2, :])):
                    link(nc.vector.tensor_scalar(part[:, i, :], src, rmask[:, 2 * i:2 * i + 1], None, ALU.mult))
                    ins = nc.vector.scalar_tensor_tensor(
                        out=tab[:, g % 2, i, :], in0=src, scalar=rmask[:, 2 * i + 1:2 * i + 2],
                        in1=part[:, i, :].bitcast(F32), op0=ALU.mult, op1=ALU.add)
                    link(ins)
                nc.vector.tensor_copy(nega[:, 0:1], nega[:, 1:2]).then_inc(tab_ready, 1)
                nc.vector.tensor_copy(fl[:, 0, 0:1], fl[:, 1, 0:1]).then_inc(fsum, 1)
                dve.wait_ge(fsum, g + 1)
                dve.wait_ge(tab_ready, g + 1)

        @block.tensor
        def _(pe):
            pe.wait_ge(loaded, 16 * 11)
            pe.wait_ge(step, marks["silu"])
            for n in range(3):
                if n:
                    pe.wait_ge(step, marks["row", n - 1])
                for c in range(DC):
                    m = nc.tensor.matmul(p_a[0:B, :], silu[:, c, :], wmod[:, c, n * 512:(n + 1) * 512],
                                         start=c == 0, stop=c == DC - 1)
                m.then_inc(modp, 1)
            for n in range(6 * DC):
                for c in range(DC):
                    m = nc.tensor.matmul(p_b[:, n * B:(n + 1) * B], wmod[:, c, n * P:(n + 1) * P], silu[:, c, :],
                                         start=c == 0, stop=c == DC - 1)
            m.then_inc(modp, 1)
            pe.wait_ge(step, marks["row", 2])
            for n in range(4):
                for c in range(DC):
                    m = nc.tensor.matmul(p_a[:, n:n + 1], wpos[:, c, n * P:(n + 1) * P], rel[:, c, 0, S - 1:S],
                                         start=c == 0, stop=c == DC - 1)
            m.then_inc(modp, 1)
            for g in range(PAIRS):
                if g:
                    pe.wait_ge(biased, 3 * g)
                for i, w, r in ((0, wpk, 0), (1, wpq, 0), (2, wpq, 1)):
                    for c in range(DC):
                        m = nc.tensor.matmul(p_t[i][:, 0:S], w[:, c, g * P:(g + 1) * P], rel[:, c, r, :],
                                             start=c == 0, stop=c == DC - 1)
                m.then_inc(tabp, 1)
                pe.wait_ge(step, marks["delta", g])
                nc.tensor.matmul(p_t[3][:, 0:S], fl[:, 0, :], delta[:, 0, :], start=True, stop=False)
                nc.tensor.matmul(p_t[3][:, 0:S], fl[:, 1, :], delta[:, 1, :], start=False,
                                 stop=True).then_inc(fp, 1)


def build_qkv(nc, d):
    with ExitStack() as ctx:
        sb, ps, sem = alloc(nc, ctx)
        ident = sb("qk_ident", [P, P])
        w_raw = sb("qk_wraw", [P, 3, DC, D])
        w_hi = sb("qk_whi", [P, 3, DC, D], F32R)
        w_lo = sb("qk_wlo", [P, 3, DC, D], F32R)
        bv = sb("qk_bv", [P, D])
        mod = sb("qk_mod", [P, B * 6 * DC])
        mb = sb("qk_mb", [P, 6, DC])
        xt = [sb(f"qk_x{u}", [P, TT, D]) for u in range(2)]
        st = sb("qk_st", [P, TT, 6])
        mv = sb("qk_mv", [P, TT, 2])
        rstd = sb("qk_rstd", [P, TT])
        power = sb("qk_power", [P, TT])
        var = sb("qk_var", [P, TT])
        hn = sb("qk_hn", [P, TT, D])
        hT = sb("qk_hT", [P, DC, T])
        h_hi = sb("qk_hhi", [P, DC, T], F32R)
        h_lo = sb("qk_hlo", [P, DC, T], F32R)
        q_hi = sb("qk_qhi", [P, 4, T], F32R)
        q_lo = sb("qk_qlo", [P, 4, T], F32R)
        v = sb("qk_v", [P, PAIRS, TT, 2, DKS])
        p_h = [ps(f"qk_ph{c}") for c in range(DC)]
        p_q = [ps(f"qk_pq{i}") for i in range(4)]
        p_v = [ps(f"qk_pv{i}") for i in range(2)]
        loaded, wsplit = sem("qk_loaded"), sem("qk_wsplit")
        power_set, v_set = sem("qk_power_set"), sem("qk_v_set")
        x_in = [sem("qk_xin0"), sem("qk_xin1")]
        stats = sem("qk_stats")
        powered, normed, transposed = sem("qk_powered"), sem("qk_normed"), sem("qk_transposed")
        modulated, split, projected, vprod = (sem("qk_modulated"), sem("qk_split"), sem("qk_projected"),
                                              sem("qk_vprod"))
        hi_ready, lo_ready, v_ready = sem("qk_hi"), sem("qk_lo"), sem("qk_v_ready")
        stored = sem("qk_stored")
        STATS = 2 * TT + 2
        STORES = 13
        block = ctx.enter_context(nc.Block())

        @block.sync
        def _(sp):
            credit(sp, [stats, powered, normed, transposed, modulated, split, projected, vprod,
                        hi_ready, lo_ready, v_ready], [stored])
            for u in range(2):
                sp.dma_start(xt[u][:, :, :], d["x"][u].rearrange("(t p) n -> p t n", p=P)).then_inc(x_in[u], 16)
            for i, w in enumerate(("wq", "wk", "wv")):
                sp.dma_start(w_raw[:, i, :, :], d[w].rearrange("(c p) n -> p c n", p=P)).then_inc(loaded, 16)
            sp.dma_start(bv[:, :], d["bv"].partition_broadcast(P)).then_inc(loaded, 16)
            sp.dma_start(mod[:, :], d["modcol"].rearrange("p b k c -> p (b k c)")).then_inc(loaded, 16)
            sp.dma_start(ident[:, :], d["ident"]).then_inc(loaded, 16)
            def load_next(b, u):
                sp.wait_ge(normed, at(TT * b + TT))
                sp.dma_start(xt[u][:, :, :], d["x"][bass.ds((b + 2) % B, 1)].squeeze(0)
                             .rearrange("(t p) n -> p t n", p=P)).then_inc(x_in[u], 16)

            load_next(0, 0)
            with sp.Fori(0, B // 2) as bb:
                for u in range(2):
                    b = bb * 2 + u
                    load_next(b + 1, 1 - u)
                    sp.wait_ge(hi_ready, at(b * 4 + 4))
                    sp.wait_ge(lo_ready, at(b * 4 + 4))
                    for i in range(4):
                        parts = (q_hi, q_lo, q_hi) if i < 2 else (q_hi, q_hi, q_lo)
                        for k, src in enumerate(parts):
                            o = d["stack"][bass.ds(b * H + 8 * (i % 2), 8), i // 2, k * DK:(k + 1) * DK]
                            sp.dma_start(o, src[:, i, :].bitcast(F32)).then_inc(stored, 16)
                    sp.wait_ge(v_ready, at(b * TT + TT))
                    sp.dma_start(d["vals"][bass.ds(b, 1)].squeeze(0), v[:, :, :, :, :]
                                 .rearrange("p h t j e -> p h (t j e)")).then_inc(stored, 16)
            sp.wait_ge(stored, dma_at(STORES * B))
            for u in range(2):
                sp.wait_ge(x_in[u], 16 * (B // 2 + 2 - u))

        @block.gpsimd
        def _(pool):
            nc.gpsimd.memset(v[:, :, :, :, :], 1.0).then_inc(v_set, 1)
            nc.gpsimd.memset(power[:, :], -0.5).then_inc(power_set, 1)
            pool.wait_ge(power_set, 1)
            with pool.Fori(0, B + 1) as b:
                pool.wait_ge(stats, at(b * STATS + STATS))
                pool.wait_ge(normed, at(b * TT))
                nc.gpsimd.tensor_tensor(rstd[:, :], var[:, :], power[:, :], ALU.pow).then_inc(powered, 1)

        @block.scalar
        def _(act):
            def modulate(b):
                act.wait_ge(transposed, at(b + 1))
                act.wait_ge(split, at(b * 4))
                for c in range(DC):
                    nc.scalar.activation(hT[:, c, :], p_h[c][:, :], ACT.Identity, scale=mb[:, 1, c:c + 1],
                                         bias=mb[:, 0, c:c + 1]).then_inc(modulated, 1)

            modulate(0)
            with act.Fori(0, B) as b:
                act.wait_ge(stored, dma_at(b * STORES))
                for i in range(4):
                    act.wait_ge(projected, at(b * 4 + i + 1))
                    nc.scalar.activation(q_hi[:, i, :], p_q[i][:, :], ACT.Identity,
                                         bias=d["qkbias"][:, i:i + 1]).then_inc(hi_ready, 1)
                modulate(b + 1)

        @block.vector
        def _(dve):
            dve.wait_ge(loaded, 16 * 6)
            dve.wait_ge(v_set, 1)
            nc.vector.tensor_copy(w_hi[:, :, :, :], w_raw[:, :, :, :]).then_inc(wsplit, 1)
            dve.wait_ge(wsplit, 1)
            nc.vector.tensor_tensor(w_lo[:, :, :, :], w_raw[:, :, :, :], w_hi[:, :, :, :].bitcast(F32),
                                    ALU.subtract).then_inc(wsplit, 1)
            def norm(b, u, n):
                dve.wait_ge(x_in[u], n * 16)
                for t in range(TT):
                    nc.vector.bn_stats(st[:, t, :], xt[u][:, t, :]).then_inc(stats, 1)
                dve.wait_ge(modulated, at(b * DC))
                dve.wait_ge(stats, at(b * STATS + TT))
                nc.vector.tensor_copy(mb[:, :, :], mod[:, bass.ds(b % B * (6 * DC), 6 * DC)]
                                      .rearrange("p (k c) -> p k c", c=DC)).then_inc(stats, 1)
                for t in range(TT):
                    nc.vector.bn_aggr(mv[:, t, :], st[:, t, :]).then_inc(stats, 1)
                dve.wait_ge(stats, at(b * STATS + 1 + 2 * TT))
                nc.vector.tensor_scalar_add(var[:, :], mv[:, :, 1], EPS).then_inc(stats, 1)
                dve.wait_ge(powered, at(b + 1))
                dve.wait_ge(transposed, at(b))
                for t in range(TT):
                    nc.vector.tensor_scalar(hn[:, t, :], xt[u][:, t, :], mv[:, t, 0:1], rstd[:, t:t + 1],
                                            ALU.subtract, ALU.mult).then_inc(normed, 1)

            norm(0, 0, 1)
            with dve.Fori(0, B // 2) as bb:
                for u in range(2):
                    b = bb * 2 + u
                    dve.wait_ge(vprod, at(b * TT))
                    dve.wait_ge(projected, at(b * 4))
                    for c in range(DC):
                        dve.wait_ge(modulated, at(b * DC + c + 1))
                        nc.vector.tensor_copy(h_hi[:, c, :], hT[:, c, :]).then_inc(split, 1)
                    dve.wait_ge(split, at(b * 4 + 2))
                    for c in range(DC):
                        nc.vector.tensor_tensor(h_lo[:, c, :], hT[:, c, :], h_hi[:, c, :].bitcast(F32),
                                                ALU.subtract).then_inc(split, 1)
                    norm(b + 1, 1 - u, bb + 1 + u)
                    dve.wait_ge(stored, dma_at(b * STORES))
                    for i in range(4):
                        dve.wait_ge(hi_ready, at(b * 4 + i + 1))
                        nc.vector.scalar_tensor_tensor(
                            out=q_lo[:, i, :], in0=p_q[i][:, :], scalar=d["qkbias"][:, i:i + 1],
                            in1=q_hi[:, i, :].bitcast(F32), op0=ALU.add, op1=ALU.subtract).then_inc(lo_ready, 1)
                    for t in range(TT):
                        dve.wait_ge(vprod, at(b * TT + 2 * (t // 2) + 2))
                        nc.vector.tensor_tensor(v[:, :, t, :, 0:DK], p_v[t // 2][:, (t % 2) * D:(t % 2) * D + D]
                                                .rearrange("p (h j e) -> p h j e", h=PAIRS, j=2),
                                                bv[:, :].rearrange("p (h j e) -> p h j e", h=PAIRS, j=2), ALU.add).then_inc(v_ready, 1)

        @block.tensor
        def _(pe):
            pe.wait_ge(loaded, 16 * 6)
            pe.wait_ge(wsplit, 2)
            def transpose(b):
                pe.wait_ge(modulated, at(b * DC))
                for t in range(TT):
                    pe.wait_ge(normed, at(b * TT + t + 1))
                    for c in range(DC):
                        m = nc.tensor.transpose(p_h[c][:, t * P:(t + 1) * P], hn[:, t, c * P:(c + 1) * P],
                                                ident[:, :])
                m.then_inc(transposed, 1)

            transpose(0)
            with pe.Fori(0, B) as b:
                pe.wait_ge(split, at(b * 4 + 4))
                for i in range(4):
                    pe.wait_ge(lo_ready, at(b * 4))
                    n0 = (i % 2) * P
                    prods = [(w, h, c) for w, h in ((w_hi, h_hi), (w_hi, h_lo), (w_lo, h_hi))
                             for c in range(DC)]
                    for n, (w, h, c) in enumerate(prods):
                        m = nc.tensor.matmul(p_q[i][:, :], w[:, i // 2, c, n0:n0 + P], h[:, c, :],
                                             start=n == 0, stop=n == len(prods) - 1)
                    m.then_inc(projected, 1)
                transpose(b + 1)
                pe.wait_ge(v_ready, at(b * TT))
                for t in range(TT):
                    prods = [(w, h, c) for w, h in ((w_hi, h_hi), (w_hi, h_lo), (w_lo, h_hi))
                             for c in range(DC)]
                    for n, (w, h, c) in enumerate(prods):
                        m = nc.tensor.matmul(p_v[t // 2][:, (t % 2) * D:(t % 2) * D + D],
                                             h[:, c, t * P:(t + 1) * P], w[:, 2, c, :],
                                             start=n == 0, stop=n == len(prods) - 1)
                    m.then_inc(vprod, 1)


def build_attention(nc, d):
    with ExitStack() as ctx:
        sb, ps, sem = alloc(nc, ctx)
        HPT = 4
        TURNS = B * H // HPT
        TILES = HPT * TT
        AHEAD = 3
        LEAD, TLEAD = TT + 2, TT
        ident = sb("at_ident", [P, P])
        tri = sb("at_tri", [P, 2, P])
        ones = sb("at_ones", [P, 2 * P])
        tri_val = sb("at_tri_val", [P, 2, TT - 1, P])
        st = [sb(f"at_st{u}", [P, 2, T], F32R) for u in range(2)]
        tab = [sb(f"at_tab{u}", [P, 2, S], F32R) for u in range(2)]
        val = [sb(f"at_val{u}", [P, TT, 2 * DKS]) for u in range(2)]
        genC = [sb(f"at_genC{i}", [P, TT, S]) for i in range(HPT)]
        genP = [sb(f"at_genP{i}", [P, TT, S]) for i in range(HPT)]
        CS = [sb(f"at_CS{i}", [P, CSW]) for i in range(HPT)]
        PS = [sb(f"at_PS{i}", [P, CSW]) for i in range(HPT)]
        scores = [sb(f"at_scores{i}", [P, T]) for i in range(2)]
        probs = [sb(f"at_probs{i}", [P, T]) for i in range(2)]
        probsT = [sb(f"at_probsT{i}", [P, TT, T]) for i in range(2)]
        negmax = sb("at_negmax", [P, TT])
        cx = [sb(f"at_cx{u}", [32 + DKS, T]) for u in range(2)]
        b_C, b_P = ps("at_bC"), ps("at_bP")
        b_S = [ps(f"at_bS{i}") for i in range(2)]
        b_T = [ps(f"at_bT{i}") for i in range(2)]
        b_X = [ps(f"at_bX{i}") for i in range(2)]
        consts, cleared, zeroed = sem("at_consts"), sem("at_cleared"), sem("at_zeroed")
        head_in = [sem(f"at_head_in{i}") for i in range(HPT)]
        val_in = [sem(f"at_val_in{u}") for u in range(2)]
        c_made, p_made, c_out, p_out = sem("at_c_made"), sem("at_p_made"), sem("at_c_out"), sem("at_p_out")
        written = [sem(f"at_written{i}") for i in range(HPT)]
        sheared = [[sem(f"at_sheared{k}{i}") for i in range(HPT)] for k in "CP"]
        filled, fixed, tri_made = sem("at_filled"), sem("at_fixed"), sem("at_tri_made")
        scored, biased, exped, turned = sem("at_scored"), sem("at_biased"), sem("at_exped"), sem("at_turned")
        copied, summed, paired = sem("at_copied"), sem("at_summed"), sem("at_paired")
        ctx_out = [sem(f"at_ctx_out{u}") for u in range(2)]
        settled = sem("at_settled")
        HEAD = 2
        block = ctx.enter_context(nc.Block())

        def rows_of(n):
            return (n // 2) % 2, slice(64 * (n % 2), 64 * (n % 2) + 64)

        def col(row_block, k):
            return SPAN + row_block * T + k

        def steps():
            for k in range(TILES):
                t = k + LEAD
                g = t - TT + 1
                yield k, t, k + TLEAD, g // TT + AHEAD, g % TT if g % TT < 2 else None

        before = {TT - 1: (AHEAD, AHEAD, 0), TT: (AHEAD, AHEAD, 1)}

        @block.sync
        def _(sp):
            credit(sp, [c_made, p_made, c_out, p_out, filled, fixed, tri_made, scored, biased, exped, turned,
                        copied, summed, paired],
                   head_in + val_in + written + sheared[0] + sheared[1] + ctx_out)
            sp.dma_start(ident[:, :], d["ident"]).then_inc(consts, 16)
            sp.dma_start(tri[:, :, :], d["tri"]).then_inc(consts, 16)
            sp.wait_ge(cleared, 1)
            for u in range(2):
                for j in range(2):
                    sp.dma_start(st[u][64 * j + 48:64 * j + 64, 0, :].bitcast(F32), d["headpad"])\
                        .then_inc(consts, 16)

            def load_head(m, n):
                u, j = (n // 2) % 2, n % 2
                sp.dma_start(st[u][64 * j:64 * j + 48, :, :].bitcast(F32),
                             d["stack"][bass.ds(m % (B * H), 1)].squeeze(0).rearrange("z r t -> r z t"))\
                    .then_inc(head_in[n % HPT], 16)
                sp.dma_start(tab[u][64 * j:64 * j + 64, :, :].bitcast(F32),
                             d["tabs"][bass.ds(m // 2 % PAIRS, 1)].squeeze(0)[64 * j:64 * j + 64])\
                    .then_inc(head_in[n % HPT], 16)

            def load_vals(pair, u):
                sp.dma_start(val[u][:, :, :].rearrange("p t e -> p (t e)"), d["vals"][bass.ds(pair // PAIRS % B, 1)].squeeze(0)
                             [:, bass.ds(pair % PAIRS, 1)].squeeze(1)).then_inc(val_in[u], 16)

            def shear(m, n):
                i = n % HPT
                size = TT * P * PITCH
                sp.wait_ge(written[i], dma_at(2 * (m // HPT + 1)))
                sp.wait_ge(biased, at(TT * (m - HPT + 1)))
                for k, (t, dst) in enumerate((("scrC", CS), ("scrP", PS))):
                    a = d[t][i, P - k:P - k + size]
                    src = bass.AP(a.tensor, a.offset, [[PITCH - 1, P], [P * PITCH, TT], [1, WIN]])
                    b = dst[i][:, :]
                    sp.dma_start(bass.AP(b.tensor, b.offset, [list(b.ap[0]), [T + SPAN, TT], [1, WIN]]),
                                 src).then_inc(sheared[k][i], 16)

            def store(pair, u):
                for j in range(2):
                    sp.dma_start(d["ctxd"][bass.ds(2 * pair + j, 1)].squeeze(0), cx[u][32 * j:32 * j + DKS, :])\
                        .then_inc(ctx_out[u], 16)

            for n in range(HPT):
                load_head(n, n)
            load_vals(0, 0)
            sp.wait_ge(zeroed, 1)
            for n in range(AHEAD):
                shear(n, n)
            with sp.Fori(0, TURNS) as it:
                for n in range(HPT):
                    m = it * HPT + n
                    sp.wait_ge(scored, at(TT * (m + 1)))
                    load_head(m + HPT, n)
                    shear(m + AHEAD, n + AHEAD)
                    if n == 0:
                        sp.wait_ge(paired, at(2 * it))
                        store((2 * it + 2 * TURNS - 1) % (2 * TURNS), 1)
                        load_vals(2 * it + 1, 1)
                    if n == 2:
                        sp.wait_ge(paired, at(2 * it + 1))
                        store(2 * it, 0)
                        load_vals(2 * it + 2, 0)
            sp.wait_ge(paired, at(2 * TURNS))
            store(2 * TURNS - 1, 1)
            for n in range(HPT):
                sp.wait_ge(head_in[n], dma_at(HEAD * (TURNS + 1)))
                for k in range(2):
                    sp.wait_ge(sheared[k][n], dma_at(TURNS + (n < AHEAD)))
                sp.wait_ge(written[n], dma_at(2 * (TURNS + 1)))
            for u in range(2):
                sp.wait_ge(val_in[u], dma_at(TURNS + 1 - u))
                sp.wait_ge(ctx_out[u], dma_at(2 * (TURNS + u)))

        @block.gpsimd
        def _(pool):
            for u in range(2):
                m = nc.gpsimd.memset(st[u][:, :, :].bitcast(F32), 0.0)
            m.then_inc(cleared, 1)
            for cs in range(HPT):
                nc.gpsimd.memset(CS[cs][:, :], 0.0)
            nc.gpsimd.memset(ones[:, :], 1.0)
            nc.gpsimd.memset(cx[0][:, :], 0.0)
            nc.gpsimd.memset(cx[1][:, :], 0.0).then_inc(zeroed, 1)
            pool.wait_ge(consts, 16 * 2)

            def fix(m, n):
                i = n % HPT
                pool.wait_ge(c_out, at(2 * m + 2))
                pool.wait_ge(p_out, at(2 * m + 2))
                pool.wait_ge(fixed, at(m))
                tables = ((CS[i], genC[i], 0), (PS[i], genP[i], S - 1))
                for k, (dst, src, c0) in enumerate(tables):
                    r = slice(1, TT) if k == 0 else slice(0, TT - 1)
                    nc.gpsimd.tensor_tensor(tri_val[:, k, :, :],
                                            tri[:, k, :].unsqueeze(1).to_broadcast([P, TT - 1, P]),
                                            src[:, r, c0:c0 + 1].to_broadcast([P, TT - 1, P]),
                                            ALU.mult).then_inc(tri_made, 1)
                pool.wait_ge(tri_made, at(2 * m + 2))
                for k, (dst, src, c0) in enumerate(tables):
                    b = dst[:, :]
                    o = bass.AP(b.tensor, b.offset + (col(1, 0) if k == 0 else col(0, P)),
                                [list(b.ap[0]), [T + P, TT - 1], [1, P]])
                    pool.wait_ge(sheared[k][i], dma_at(m // HPT + 1))
                    last = nc.gpsimd.tensor_tensor(o, o, tri_val[:, k, :, :], ALU.add)
                last.then_inc(fixed, 1)

            for n in range(AHEAD):
                fix(n, n)
            with pool.Fori(0, TURNS) as it:
                for n in range(HPT):
                    fix(it * HPT + n + AHEAD, n + AHEAD)

        @block.scalar
        def _(act):
            def p_copy(m, n, half):
                act.wait_ge(p_made, at(2 * m + half + 1))
                if half == 0:
                    act.wait_ge(fixed, at(m - HPT + 1))
                    act.wait_ge(filled, at(m - HPT + 1))
                nc.scalar.activation(genP[n % HPT][:, 2 * half:2 * half + 2, :],
                                     b_P[:, :].rearrange("p (a s) -> p a s", a=2), ACT.Copy).then_inc(p_out, 1)

            def write(m, n):
                i = n % HPT
                size = TT * P * PITCH
                act.wait_ge(c_out, at(2 * m + 2))
                act.wait_ge(p_out, at(2 * m + 2))
                for t, src in (("scrC", genC), ("scrP", genP)):
                    act.dma_start(d[t][i, P:P + size].rearrange("(t p n) -> p t n", p=P, n=PITCH)[:, :, 0:S],
                                  src[i][:, :, :]).then_inc(written[i], 16)

            def exp(it, t):
                n, qb = t // TT, t % TT
                act.wait_ge(biased, at(it * TILES + t + 1))
                act.wait_ge(turned, at(it * TILES + t - 1))
                nc.scalar.activation(probs[t % 2][:, :], scores[t % 2][:, :], ACT.Exp,
                                     bias=negmax[:, qb:qb + 1], scale=-1.0).then_inc(exped, 1)

            def copy(it, tr):
                n, qb = tr // TT, tr % TT
                act.wait_ge(turned, at(it * TILES + tr + 1))
                if qb == 0:
                    act.wait_ge(summed, at(it * TILES + TT * (n - 1)))
                nc.scalar.activation(probsT[n % 2][:, :, qb * P:(qb + 1) * P], b_T[tr % 2][:, :]
                                     .rearrange("p (k q) -> p k q", q=P), ACT.Copy).then_inc(copied, 1)

            for n in range(AHEAD):
                for half in range(2):
                    p_copy(n, n, half)
                write(n, n)
            for t in range(LEAD):
                exp(0, t)
                if t in before:
                    p_copy(*before[t])
                if t >= 2:
                    copy(0, t - 2)
                if t in before and before[t][2] == 1:
                    write(*before[t][:2])
            with act.Fori(0, TURNS) as it:
                for k, t, tr, g, half in steps():
                    exp(it, t)
                    if half is not None:
                        p_copy(it * HPT + g, g, half)
                    copy(it, tr)
                    if half == 1:
                        write(it * HPT + g, g)

        @block.vector
        def _(dve):
            def c_copy(m, n, half):
                dve.wait_ge(c_made, at(2 * m + half + 1))
                if half == 0:
                    dve.wait_ge(fixed, at(m - HPT + 1))
                nc.vector.tensor_copy(genC[n % HPT][:, 2 * half:2 * half + 2, :],
                                      b_C[:, :].rearrange("p (a s) -> p a s", a=2)).then_inc(c_out, 1)

            def fill(m, n):
                i = n % HPT
                dve.wait_ge(c_out, at(2 * m + 2))
                dve.wait_ge(p_out, at(2 * m + 2))
                dve.wait_ge(scored, at(TT * (m - HPT + 1)))
                dve.sem_inc(settled, 1)
                for k, (dst, src, c0) in enumerate(((CS[i], genC[i], 0), (PS[i], genP[i], S - 1))):
                    for r in ((2, 3) if k == 0 else (0, 1)):
                        lo, hi = (0, (r - 1) * P) if k == 0 else ((r + 2) * P, T)
                        last = nc.vector.tensor_scalar(dst[:, col(r, lo):col(r, hi)], ones[:, 0:hi - lo],
                                                       src[:, r, c0:c0 + 1], None, ALU.mult)
                last.then_inc(filled, 1)

            def bias(it, t):
                n, qb = t // TT, t % TT
                dve.wait_ge(scored, at(it * TILES + t + 1))
                dve.wait_ge(exped, at(it * TILES + t - 1))
                if qb == 0:
                    dve.wait_ge(filled, at(it * HPT + n + 1))
                dve.sem_inc(settled, 1)
                nc.vector.tensor_tensor_reduce(
                    out=scores[t % 2][:, :], in0=b_S[t % 2][:, :], in1=CS[n % HPT][:, col(qb, 0):col(qb, T)],
                    scale=-SCALE, scalar=BIG, op0=ALU.add, op1=ALU.min,
                    accum_out=negmax[:, qb:qb + 1]).then_inc(biased, 1)

            dve.wait_ge(zeroed, 1)
            for n in range(AHEAD):
                for half in range(2):
                    c_copy(n, n, half)
                fill(n, n)
            for t in range(LEAD):
                bias(0, t)
                if t in before:
                    c_copy(*before[t])
                    if before[t][2] == 1:
                        fill(*before[t][:2])
            with dve.Fori(0, TURNS) as it:
                for k, t, tr, g, half in steps():
                    bias(it, t)
                    if half is not None:
                        c_copy(it * HPT + g, g, half)
                    if half == 1:
                        fill(it * HPT + g, g)
                    if k % (2 * TT) == 2 * TT - 1:
                        u = k // (2 * TT)
                        dve.wait_ge(summed, at(it * TILES + k + 1))
                        dve.wait_ge(ctx_out[u], dma_at(2 * (it + u)))
                        nc.vector.tensor_copy(cx[u][:, :], b_X[u][0:32 + DKS, :]).then_inc(paired, 1)

        @block.tensor
        def _(pe):
            def generate(m, n, half):
                u, rows = rows_of(n)
                if half == 0:
                    pe.wait_ge(head_in[n % HPT], dma_at(HEAD * (m // HPT + 1)))
                for bank, made, out, k in ((b_C, c_made, c_out, 0), (b_P, p_made, p_out, 1)):
                    pe.wait_ge(out, at(2 * m + half))
                    for a in range(2):
                        blk = 2 * half + a
                        mm = nc.tensor.matmul(bank[:, a * S:(a + 1) * S], st[u][rows, k, blk * P:(blk + 1) * P],
                                              tab[u][rows, k, :], start=True, stop=True)
                    mm.then_inc(made, 1)

            def score(it, t):
                n, qb = t // TT, t % TT
                u, rows = rows_of(n)
                if qb == 0:
                    pe.wait_ge(fixed, at(it * HPT + n + 1))
                    pe.wait_ge(filled, at(it * HPT + n + 1))
                pe.wait_ge(biased, at(it * TILES + t - 1))
                nc.tensor.matmul(b_S[t % 2][:, :], st[u][rows, 0, qb * P:(qb + 1) * P], st[u][rows, 1, :],
                                 start=True, stop=True)
                for kb in range(min(qb + 2, TT)):
                    c = col(kb, qb * P)
                    mm = nc.tensor.matmul(b_S[t % 2][:, kb * P:(kb + 1) * P], PS[n % HPT][:, c:c + P],
                                          ident[:, :], start=False, stop=True, skip_group_check=True)
                mm.then_inc(scored, 1)

            def turn(it, tr):
                pe.wait_ge(exped, at(it * TILES + tr + 1))
                pe.wait_ge(copied, at(it * TILES + tr - 1))
                for kb in range(TT):
                    mm = nc.tensor.transpose(b_T[tr % 2][:, kb * P:(kb + 1) * P],
                                             probs[tr % 2][:, kb * P:(kb + 1) * P], ident[:, :])
                mm.then_inc(turned, 1)

            pe.wait_ge(consts, 16 * 6)
            for n in range(AHEAD):
                for half in range(2):
                    generate(n, n, half)
            for t in range(LEAD):
                score(0, t)
                if t in before:
                    generate(*before[t])
                if t >= 2:
                    turn(0, t - 2)
            with pe.Fori(0, TURNS) as it:
                for k, t, tr, g, half in steps():
                    score(it, t)
                    turn(it, tr)
                    if half is not None:
                        generate(it * HPT + g, g, half)
                    n, kb = k // TT, k % TT
                    if kb == 0:
                        pe.wait_ge(copied, at(it * TILES + k + TT))
                    if k % (2 * TT) == 0:
                        pe.wait_ge(paired, at(2 * it + k // (2 * TT) - 1))
                        pe.wait_ge(val_in[n // 2], dma_at(it + 1))
                    r, rows = 32 * (n % 2), DKS if n % 2 else 32
                    nc.tensor.matmul(b_X[n // 2][r:r + rows, :],
                                     val[n // 2][:, kb, DKS * (n % 2):DKS * (n % 2) + rows],
                                     probsT[n % 2][:, kb, :], start=kb == 0, stop=kb == TT - 1)\
                        .then_inc(summed, 1)


def build_post(nc, d):
    with ExitStack() as ctx:
        sb, ps, sem = alloc(nc, ctx)
        GROUPS = P // H
        GT = T // GROUPS
        ident = sb("po_ident", [P, P])
        wo = sb("po_wo", [P, DC, D])
        wo_hi = sb("po_wohi", [P, DC, D], F32R)
        wo_lo = sb("po_wolo", [P, DC, D], F32R)
        bo = sb("po_bo", [P, D])
        wr = sb("po_wr", [P, DC, E])
        br = sb("po_br", [P, E])
        mod = sb("po_mod", [P, B * 6 * DC])
        power = sb("po_power", [P, TT])
        spread = sb("po_spread", [P, GROUPS, DC, P])
        ct = [sb(f"po_ctx{u}", [P, DC, T]) for u in range(2)]
        sums = [sb(f"po_sums{u}", [P, GT]) for u in range(2)]
        inv_sum = sb("po_inv_sum", [P, GT])
        cn = sb("po_cn", [P, DC, T])
        xt = [sb(f"po_xt{u}", [P, TT, D]) for u in range(2)]
        ga = [sb(f"po_ga{u}", [P, D]) for u in range(2)]
        mb = sb("po_mb", [P, 6, DC])
        c_hi = sb("po_chi", [P, DC, T], F32R)
        c_lo = sb("po_clo", [P, DC, T], F32R)
        bias = sb("po_bias", [P, D])
        base = sb("po_base", [P, TT, D])
        att = sb("po_att", [P, TT, D])
        x1 = [sb(f"po_x1_{u}", [P, TT, D]) for u in range(2)]
        st = sb("po_st", [P, TT, 6])
        mv = sb("po_mv", [P, TT, 2])
        var = sb("po_var", [P, TT])
        rstd = sb("po_rstd", [P, TT])
        hn = sb("po_hn", [P, TT, D])
        hT = sb("po_hT", [P, DC, T])
        logits = sb("po_logits", [P, TT, E])
        ex = sb("po_ex", [P, TT, E])
        den = sb("po_den", [P, TT, E])
        aff = sb("po_aff", [P, TT, E])
        top = sb("po_top", [P, TT, TOPK])
        rest = sb("po_rest", [P, TT, E])
        sel = sb("po_sel", [P, TT, E])
        total = sb("po_total", [P, TT])
        safe = sb("po_safe", [P, TT])
        inv = sb("po_inv", [P, TT])
        wts = sb("po_wts", [P, TT, P])
        wT = sb("po_wT", [EA, T])
        p_c = [ps(f"po_pc{c}") for c in range(DC)]
        p_a = [ps(f"po_pa{i}") for i in range(2)]
        p_h = [ps(f"po_ph{c}") for c in range(DC)]
        p_l, p_w = ps("po_pl"), ps("po_pw")
        loaded, wsplit = sem("po_loaded"), sem("po_wsplit")
        power_set, wts_set = sem("po_power_set"), sem("po_wts_set")
        settled = sem("po_settled")
        ctx_in = [sem("po_ctx_in0"), sem("po_ctx_in1")]
        x_in = [sem("po_x_in0"), sem("po_x_in1")]
        inverted, spreaded, normalised = sem("po_inverted"), sem("po_spreaded"), sem("po_normalised")
        rounded, split = sem("po_rounded"), sem("po_split")
        based, multiplied, added = sem("po_based"), sem("po_multiplied"), sem("po_added")
        scaled = sem("po_scaled")
        stats, powered, normed = sem("po_stats"), sem("po_powered"), sem("po_normed")
        h_turned, modulated = sem("po_h_turned"), sem("po_modulated")
        scored, biased, exped = sem("po_scored"), sem("po_biased"), sem("po_exped")
        routed = sem("po_routed")
        w_turned, w_out = sem("po_w_turned"), sem("po_w_out")
        x1_stored = [sem("po_x1_stored0"), sem("po_x1_stored1")]
        h_stored, w_stored = sem("po_h_stored"), sem("po_w_stored")
        STATS = 2 * TT + 2
        ROUTED = 2 + 2 * TT + 5
        CTX = DC + 1
        block = ctx.enter_context(nc.Block())

        @block.sync
        def _(sp):
            credit(sp, [inverted, spreaded, normalised, rounded, split, based, multiplied, added, scaled, stats, powered, normed,
                        h_turned, modulated, scored, biased, exped, routed, w_turned, w_out],
                   x1_stored + [h_stored, w_stored])

            def load_ctx(b, u):
                for c in range(DC):
                    heads = H // DC
                    sp.dma_start(ct[u][:, c, :], d["ctxd"][bass.ds(b * H + c * heads, heads), 0:DK])\
                        .then_inc(ctx_in[u], 16)
                sp.dma_start(sums[u][:, :], d["ctxd"][bass.ds(b * H, H), DK]
                             .rearrange("h (g t) -> h g t", g=GROUPS)).then_inc(ctx_in[u], 16)

            def load_x(b, u):
                sp.dma_start(xt[u][:, :, :], d["x"][bass.ds(b, 1)].squeeze(0)
                             .rearrange("(t p) n -> p t n", p=P)).then_inc(x_in[u], 16)
                sp.dma_start(ga[u][:, :], d["modrow"][bass.ds(b, 1)].squeeze(0)[2 * D:3 * D]
                             .partition_broadcast(P)).then_inc(x_in[u], 16)

            for u in range(2):
                load_ctx(u, u)
                load_x(u, u)
            sp.dma_start(ident[:, :], d["ident"]).then_inc(loaded, 16)
            sp.dma_start(spread[:, :, :], d["spread"]).then_inc(loaded, 16)
            sp.dma_start(wo[:, :, :], d["wo"].rearrange("(c p) n -> p c n", p=P)).then_inc(loaded, 16)
            sp.dma_start(bo[:, :], d["bo"].partition_broadcast(P)).then_inc(loaded, 16)
            sp.dma_start(wr[:, :, :], d["wr"].rearrange("(c p) n -> p c n", p=P)).then_inc(loaded, 16)
            sp.dma_start(br[:, :], d["br"].partition_broadcast(P)).then_inc(loaded, 16)
            sp.dma_start(mod[:, :], d["modcol"].rearrange("p b k c -> p (b k c)")).then_inc(loaded, 16)
            def after_projection(b, u):
                sp.wait_ge(normalised, at(b * DC + DC))
                load_ctx((b + 2) % B, u)
                sp.wait_ge(based, at(2 * b + 2))
                sp.wait_ge(scaled, at(2 * b + 2))
                load_x((b + 2) % B, u)
                sp.wait_ge(added, at(2 * b + 2))
                sp.dma_start(d["x1"][bass.ds(b % B, 1)].squeeze(0), x1[u][:, :, :]).then_inc(x1_stored[u], 16)

            after_projection(0, 0)
            with sp.Fori(0, B // 2) as bb:
                for u in range(2):
                    b = bb * 2 + u
                    sp.wait_ge(modulated, at(DC * b + DC))
                    sp.dma_start(d["h2T"][bass.ds(b, 1)].squeeze(0), hT[:, :, :]).then_inc(h_stored, 16)
                    after_projection(b + 1, 1 - u)
                    sp.wait_ge(w_out, at(b + 1))
                    sp.dma_start(d["wT"][:, bass.ds(b * T, T)], wT[:, :]).then_inc(w_stored, 16)
            for s in (h_stored, w_stored):
                sp.wait_ge(s, dma_at(B))
            for u in range(2):
                loads = B // 2 + 2 - u
                sp.wait_ge(x1_stored[u], dma_at(loads - 1))
                sp.wait_ge(ctx_in[u], 16 * CTX * loads)
                sp.wait_ge(x_in[u], 16 * 2 * loads)

        @block.gpsimd
        def _(pool):
            nc.gpsimd.memset(power[:, :], -0.5).then_inc(power_set, 1)
            pool.wait_ge(power_set, 1)
            pool.wait_ge(loaded, 16 * 7)
            def make_base(b, u, n):
                pool.wait_ge(x_in[u], n * 32)
                nc.gpsimd.tensor_tensor(bias[:, :], bo[:, :], ga[u][:, :], ALU.mult).then_inc(based, 1)
                pool.wait_ge(based, at(2 * b + 1))
                pool.wait_ge(added, at(2 * b))
                nc.gpsimd.tensor_tensor(base[:, :, :], xt[u][:, :, :],
                                        bias[:, :].unsqueeze(1).to_broadcast([P, TT, D]),
                                        ALU.add).then_inc(based, 1)

            make_base(0, 0, 1)
            with pool.Fori(0, B // 2) as bb:
                for u in range(2):
                    b = bb * 2 + u
                    pool.wait_ge(stats, at(b * STATS + STATS))
                    pool.wait_ge(normed, at(b * TT))
                    nc.gpsimd.tensor_tensor(rstd[:, :], var[:, :], power[:, :], ALU.pow).then_inc(powered, 1)
                    make_base(b + 1, 1 - u, bb + 1 + u)

        @block.scalar
        def _(act):
            def round_context(b):
                act.wait_ge(multiplied, at(b * 2))
                for c in range(DC):
                    act.wait_ge(normalised, at(b * DC + c + 1))
                    nc.scalar.activation(c_hi[:, c, :], cn[:, c, :], ACT.Copy).then_inc(rounded, 1)

            round_context(0)
            with act.Fori(0, B) as b:
                round_context(b + 1)
                act.wait_ge(h_turned, at(b + 1))
                act.wait_ge(scored, at(b))
                act.wait_ge(h_stored, dma_at(b))
                for c in range(DC):
                    nc.scalar.activation(hT[:, c, :], p_h[c][:, :], ACT.Identity, scale=mb[:, 4, c:c + 1],
                                         bias=mb[:, 3, c:c + 1]).then_inc(modulated, 1)
                act.wait_ge(biased, at(b + 1))
                act.wait_ge(routed, at(b * ROUTED))
                nc.scalar.activation(ex[:, :, :], logits[:, :, :], ACT.Exp, scale=-1.0).then_inc(exped, 1)
                act.wait_ge(w_turned, at(b + 1))
                act.wait_ge(w_stored, dma_at(b))
                nc.scalar.activation(wT[:, :], p_w[0:EA, :], ACT.Copy).then_inc(w_out, 1)

        @block.vector
        def _(dve):
            nc.vector.memset(wts[:, :, :], 1.0).then_inc(wts_set, 1)
            dve.wait_ge(loaded, 16 * 7)
            nc.vector.tensor_copy(wo_hi[:, :, :], wo[:, :, :]).then_inc(wsplit, 1)
            dve.wait_ge(wsplit, 1)
            dve.wait_ge(wts_set, 1)
            nc.vector.tensor_tensor(wo_lo[:, :, :], wo[:, :, :], wo_hi[:, :, :].bitcast(F32),
                                    ALU.subtract).then_inc(wsplit, 1)
            def invert(b, u, n):
                dve.wait_ge(ctx_in[u], n * (16 * CTX))
                dve.wait_ge(spreaded, at(b))
                nc.vector.reciprocal(inv_sum[:, :], sums[u][:, :]).then_inc(inverted, 1)

            def normalise(b, u):
                dve.wait_ge(spreaded, at(b + 1))
                dve.wait_ge(split, at(b * DC))
                for c in range(DC):
                    nc.vector.tensor_tensor(cn[:, c, :], ct[u][:, c, :], p_c[c][:, :],
                                            ALU.mult).then_inc(normalised, 1)

            def project(b, u, n):
                dve.wait_ge(multiplied, at(b * 2))
                for c in range(DC):
                    dve.wait_ge(rounded, at(b * DC + c + 1))
                    nc.vector.tensor_tensor(c_lo[:, c, :], cn[:, c, :], c_hi[:, c, :].bitcast(F32),
                                            ALU.subtract).then_inc(split, 1)
                dve.wait_ge(based, at(2 * b + 2))
                for i in range(2):
                    two = slice(2 * i, 2 * i + 2)
                    dve.wait_ge(multiplied, at(2 * b + i + 1))
                    dve.wait_ge(added, at(2 * b))
                    nc.vector.tensor_tensor(att[:, two, :], p_a[i][:, :].rearrange("p (t n) -> p t n", n=D),
                                            ga[u][:, :].unsqueeze(1).to_broadcast([P, 2, D]),
                                            ALU.mult).then_inc(scaled, 1)
                dve.wait_ge(x1_stored[u], dma_at(n - 1))
                dve.wait_ge(normed, at((b - 1) * TT))
                for i in range(2):
                    two = slice(2 * i, 2 * i + 2)
                    dve.wait_ge(scaled, at(2 * b + i + 1))
                    nc.vector.tensor_tensor(x1[u][:, two, :], att[:, two, :], base[:, two, :],
                                            ALU.add).then_inc(added, 1)

            invert(0, 0, 1)
            normalise(0, 0)
            project(0, 0, 1)
            invert(1, 1, 1)
            with dve.Fori(0, B // 2) as bb:
                for u in range(2):
                    b = bb * 2 + u
                    for t in range(TT):
                        if t % 2 == 0:
                            dve.wait_ge(added, at(2 * b + t // 2 + 1))
                        nc.vector.bn_stats(st[:, t, :], x1[u][:, t, :]).then_inc(stats, 1)
                    dve.wait_ge(modulated, at(b * DC))
                    dve.wait_ge(stats, at(b * STATS + TT))
                    nc.vector.tensor_copy(mb[:, :, :], mod[:, bass.ds(b * (6 * DC), 6 * DC)]
                                          .rearrange("p (k c) -> p k c", c=DC)).then_inc(stats, 1)
                    for t in range(TT):
                        nc.vector.bn_aggr(mv[:, t, :], st[:, t, :]).then_inc(stats, 1)
                    dve.wait_ge(stats, at(b * STATS + 1 + 2 * TT))
                    nc.vector.tensor_scalar_add(var[:, :], mv[:, :, 1], EPS).then_inc(stats, 1)
                    normalise(b + 1, 1 - u)
                    dve.wait_ge(powered, at(b + 1))
                    dve.wait_ge(h_turned, at(b))
                    for t in range(TT):
                        nc.vector.tensor_scalar(hn[:, t, :], x1[u][:, t, :], mv[:, t, 0:1], rstd[:, t:t + 1],
                                                ALU.subtract, ALU.mult).then_inc(normed, 1)
                    project(b + 1, 1 - u, bb + 1 + u)
                    invert(b + 2, u, bb + 2)
                    dve.wait_ge(scored, at(b + 1))
                    dve.wait_ge(exped, at(b))
                    nc.vector.tensor_tensor(logits[:, :, :], p_l[:, 0:TT * E].rearrange("p (t e) -> p t e", e=E),
                                            br[:, :].unsqueeze(1).to_broadcast([P, TT, E]),
                                            ALU.add).then_inc(biased, 1)

                    def ready(n):
                        dve.wait_ge(routed, at(b * ROUTED + n))

                    dve.wait_ge(exped, at(b + 1))
                    nc.vector.tensor_scalar_add(den[:, :, :], ex[:, :, :], 1.0).then_inc(routed, 1)
                    ready(1)
                    nc.vector.reciprocal(aff[:, :, :], den[:, :, :]).then_inc(routed, 1)
                    ready(2)
                    dve.sem_inc(settled, 1)
                    for t in range(TT):
                        nc.vector.max(top[:, t, :], aff[:, t, :]).then_inc(routed, 1)
                    for t in range(TT):
                        ready(2 + t + 1)
                        dve.sem_inc(settled, 1)
                        nc.vector.match_replace(rest[:, t, :], top[:, t, :], aff[:, t, :], 0.0).then_inc(routed, 1)
                    ready(2 + 2 * TT)
                    nc.vector.tensor_tensor(sel[:, :, :], aff[:, :, :], rest[:, :, :], ALU.subtract)\
                        .then_inc(routed, 1)
                    nc.vector.tensor_reduce(total[:, :], top[:, :, :], mybir.AxisListType.X, ALU.add)\
                        .then_inc(routed, 1)
                    ready(2 + 2 * TT + 2)
                    nc.vector.tensor_scalar_add(safe[:, :], total[:, :], 1e-9).then_inc(routed, 1)
                    ready(2 + 2 * TT + 3)
                    nc.vector.reciprocal(inv[:, :], safe[:, :]).then_inc(routed, 1)
                    ready(2 + 2 * TT + 4)
                    dve.wait_ge(w_turned, at(b))
                    nc.vector.tensor_tensor(wts[:, :, 0:E], sel[:, :, :],
                                            inv[:, :].unsqueeze(2).to_broadcast([P, TT, E]),
                                            ALU.mult).then_inc(routed, 1)

        @block.tensor
        def _(pe):
            pe.wait_ge(loaded, 16 * 7)
            pe.wait_ge(wsplit, 2)
            def spread_inverses(b):
                pe.wait_ge(inverted, at(b + 1))
                pe.wait_ge(normalised, at(b * DC))
                for c in range(DC):
                    for g in range(GROUPS):
                        m = nc.tensor.matmul(p_c[c][:, g * GT:(g + 1) * GT], spread[:, g, c, :], inv_sum[:, :],
                                             start=True, stop=True)
                m.then_inc(spreaded, 1)

            def project(b):
                pe.wait_ge(rounded, at(b * DC + DC))
                pe.wait_ge(split, at(b * DC + DC))
                pe.wait_ge(scaled, at(2 * b))
                for i in range(2):
                    for t in (2 * i, 2 * i + 1):
                        prods = [(h, w, c) for h, w in ((c_hi, wo_hi), (c_hi, wo_lo), (c_lo, wo_hi))
                                 for c in range(DC)]
                        for n, (h, w, c) in enumerate(prods):
                            m = nc.tensor.matmul(p_a[i][:, (t % 2) * D:(t % 2) * D + D],
                                                 h[:, c, t * P:(t + 1) * P], w[:, c, :],
                                                 start=n == 0, stop=n == len(prods) - 1)
                    m.then_inc(multiplied, 1)

            spread_inverses(0)
            project(0)
            spread_inverses(1)
            with pe.Fori(0, B) as b:
                pe.wait_ge(modulated, at(b * DC))
                for t in range(TT):
                    pe.wait_ge(normed, at(b * TT + t + 1))
                    for c in range(DC):
                        m = nc.tensor.transpose(p_h[c][:, t * P:(t + 1) * P], hn[:, t, c * P:(c + 1) * P],
                                                ident[:, :])
                m.then_inc(h_turned, 1)
                project(b + 1)
                pe.wait_ge(modulated, at(b * DC + DC))
                pe.wait_ge(biased, at(b))
                for t in range(TT):
                    for c in range(DC):
                        m = nc.tensor.matmul(p_l[:, t * E:(t + 1) * E], hT[:, c, t * P:(t + 1) * P],
                                             wr[:, c, :], start=c == 0, stop=c == DC - 1)
                m.then_inc(scored, 1)
                spread_inverses(b + 2)
                pe.wait_ge(routed, at(b * ROUTED + ROUTED))
                pe.wait_ge(w_out, at(b))
                for t in range(TT):
                    m = nc.tensor.transpose(p_w[:, t * P:(t + 1) * P], wts[:, t, :], ident[:, :])
                m.then_inc(w_turned, 1)


def build_experts(nc, d):
    with ExitStack() as ctx:
        sb, ps, sem = alloc(nc, ctx)
        HALVES = BLK // T
        EPT = 3
        TURNS = EA // EPT
        UNITS = EPT * HALVES
        PAR = HALVES * DC
        bd = sb("ex_bd", [EA, D])
        h_raw = sb("ex_hraw", [P, PAR, T])
        h_hi = sb("ex_hhi", [P, 2 * PAR, T], F32R)
        h_lo = sb("ex_hlo", [P, 2 * PAR, T], F32R)
        raw = [sb(f"ex_raw{j}", [P, WCOLS + 2]) for j in range(EPT)]
        w_hi = [sb(f"ex_whi{j}", [P, WCOLS], F32R) for j in range(EPT)]
        w_lo = [sb(f"ex_wlo{j}", [P, WCOLS], F32R) for j in range(EPT)]
        share = [sb(f"ex_share{j}", [P, BLK]) for j in range(EPT)]
        silu = [sb(f"ex_silu{i}", [P, T]) for i in range(2)]
        gated = [sb(f"ex_gated{i}", [P, T]) for i in range(2)]
        hid = [sb(f"ex_hid{i}", [P, T]) for i in range(2)]
        hid_hi = [sb(f"ex_hidhi{i}", [P, T], F32R) for i in range(2)]
        hid_lo = [sb(f"ex_hidlo{i}", [P, T], F32R) for i in range(2)]
        wT = sb("ex_wT", [EA, BLK])
        x1 = sb("ex_x1", [P, HALVES * TT, D])
        gb = sb("ex_gb", [P, HALVES, D])
        scaled = sb("ex_scaled", [P, HALVES * TT, D])
        out = sb("ex_out", [P, HALVES * TT, D])
        p_o = [ps(f"ex_po{i}") for i in range(4)]
        p_g = [ps(f"ex_pg{i}") for i in range(2)]
        p_u = [ps(f"ex_pu{i}") for i in range(2)]
        bd_in, h_in, wT_in, res_in = sem("ex_bd_in"), sem("ex_h_in"), sem("ex_wT_in"), sem("ex_res_in")
        w_in = [sem(f"ex_w_in{j}") for j in range(EPT)]
        w_rounded, w_split, h_split = sem("ex_w_rounded"), sem("ex_w_split"), sem("ex_h_split")
        gate_made, up_made, started, summed = (sem("ex_gate_made"), sem("ex_up_made"), sem("ex_started"),
                                               sem("ex_summed"))
        silued, steps, rounded, split = sem("ex_silued"), sem("ex_steps"), sem("ex_rounded"), sem("ex_split")
        scale_done, out_ready, out_stored = sem("ex_scale_done"), sem("ex_out_ready"), sem("ex_out_stored")
        block = ctx.enter_context(nc.Block())

        @block.sync
        def _(sp):
            credit(sp, [w_rounded, w_split, h_split, gate_made, up_made, started, summed, silued, steps, rounded,
                        split, scale_done, out_ready], w_in + [h_in, wT_in, res_in, out_stored])
            sp.dma_start(bd[:, :], d["bd"]).then_inc(bd_in, 16)

            def load_weights(x, j):
                e, blk = x % EA, x // EA % NBLK
                sp.dma_start(raw[j][:, :], d["wexp"][bass.ds(e, 1)].squeeze(0)).then_inc(w_in[j], 16)
                sp.dma_start(share[j][:, :], d["wT"][bass.ds(e, 1)].squeeze(0)[bass.ds(blk * BLK, BLK)]
                             .partition_broadcast(P)).then_inc(w_in[j], 16)

            def load_hidden(blk):
                sp.dma_start(h_raw[:, :, :].rearrange("p (h c) t -> p h (c t)", c=DC),
                             d["h2T"][bass.ds(blk * HALVES, HALVES)].rearrange("h p c t -> p h (c t)"))\
                    .then_inc(h_in, 16)

            def load_wT(blk):
                sp.dma_start(wT[:, :], d["wT"][:, bass.ds(blk * BLK, BLK)]).then_inc(wT_in, 16)

            load_hidden(0)
            for j in range(EPT):
                load_weights(j, j)
            load_wT(0)
            with sp.Fori(0, NBLK) as blk:
                sp.wait_ge(h_split, at(2 * blk + 2))
                load_hidden((blk + 1) % NBLK)
                sp.wait_ge(started, at(4 * blk + 4))
                load_wT((blk + 1) % NBLK)
                sp.wait_ge(out_ready, at(4 * blk))
                sp.dma_start(x1[:, :, :].rearrange("p (h t) n -> p h (t n)", t=TT),
                             d["x1"][bass.ds(blk * HALVES, HALVES)].rearrange("h p t n -> p h (t n)"))\
                    .then_inc(res_in, 16)
                for h in range(HALVES):
                    sp.dma_start(gb[:, h, :], d["modrow"][bass.ds(blk * HALVES + h, 1)].squeeze(0)
                                 [5 * D:6 * D].partition_broadcast(P)).then_inc(res_in, 16)
                with sp.Fori(0, TURNS) as turn:
                    for j in range(EPT):
                        x = blk * EA + turn * EPT + j
                        sp.wait_ge(steps, at(4 * x + 4))
                        load_weights(x + EPT, j)
                for i in range(4):
                    sp.wait_ge(out_ready, at(4 * blk + i + 1))
                    sp.dma_start(d["out"][bass.ds(blk * HALVES + i // 2, 1)].squeeze(0)
                                 .rearrange("(t p) n -> p t n", p=P)[:, 2 * (i % 2):2 * (i % 2) + 2, :],
                                 out[:, 2 * i:2 * i + 2, :]).then_inc(out_stored, 16)
            sp.wait_ge(out_stored, dma_at(4 * NBLK))
            sp.wait_ge(h_in, dma_at(NBLK + 1))
            sp.wait_ge(wT_in, dma_at(NBLK + 1))
            for j in range(EPT):
                sp.wait_ge(w_in[j], dma_at(2 * (NBLK * TURNS + 1)))

        @block.gpsimd
        def _(pool):
            def split_hidden(blk):
                s = bass.ds(blk % 2 * PAR, PAR)
                pool.wait_ge(h_in, dma_at(blk + 1))
                nc.gpsimd.tensor_copy(h_hi[:, s, :], h_raw[:, :, :]).then_inc(h_split, 1)
                pool.wait_ge(h_split, at(2 * blk + 1))
                nc.gpsimd.tensor_tensor(h_lo[:, s, :], h_raw[:, :, :], h_hi[:, s, :].bitcast(F32),
                                        ALU.subtract).then_inc(h_split, 1)

            def split_weights(x, j):
                pool.wait_ge(w_rounded, at(x + 1))
                nc.gpsimd.tensor_tensor(w_lo[j][:, :], raw[j][:, 0:WCOLS], w_hi[j][:, :].bitcast(F32),
                                        ALU.subtract).then_inc(w_split, 1)

            split_hidden(0)
            for j in range(2):
                split_weights(j, j)
            with pool.Fori(0, NBLK) as blk:
                pool.wait_ge(started, at(4 * blk + 4))
                split_hidden(blk + 1)
                with pool.Fori(0, TURNS) as turn:
                    for j in range(EPT):
                        split_weights(blk * EA + turn * EPT + j + 2, (j + 2) % EPT)
                pool.wait_ge(res_in, dma_at(3 * blk + 3))
                pool.wait_ge(out_stored, dma_at(4 * blk))
                for i in range(4):
                    two = slice(2 * i, 2 * i + 2)
                    pool.wait_ge(scale_done, at(4 * blk + i + 1))
                    nc.gpsimd.tensor_tensor(out[:, two, :], scaled[:, two, :], x1[:, two, :],
                                            ALU.add).then_inc(out_ready, 1)

        @block.scalar
        def _(act):
            def round_weights(x, j, turns):
                act.wait_ge(w_in[j], dma_at(2 * turns))
                act.wait_ge(summed, at(2 * x - 4))
                nc.scalar.activation(w_hi[j][:, :], raw[j][:, 0:WCOLS], ACT.Copy).then_inc(w_rounded, 1)

            for j in range(2):
                round_weights(j, j, 1)
            with act.Fori(0, NBLK) as blk:
                with act.Fori(0, TURNS) as turn:
                    for j in range(EPT):
                        x = blk * EA + turn * EPT + j
                        for h in range(HALVES):
                            n = 2 * x + h
                            act.wait_ge(gate_made, at(n + 1))
                            act.wait_ge(steps, at(2 * n - 3))
                            nc.scalar.activation(silu[h][:, :], p_g[h][:, :], ACT.Silu,
                                                 bias=raw[j][:, WCOLS:WCOLS + 1]).then_inc(silued, 1)
                            act.wait_ge(steps, at(2 * n + 2))
                            act.wait_ge(summed, at(n - 1))
                            nc.scalar.activation(hid_hi[h][:, :], hid[h][:, :], ACT.Copy).then_inc(rounded, 1)
                            if h == 0:
                                round_weights(x + 2, (j + 2) % EPT,
                                              blk * TURNS + turn + (1 if j == 0 else 2))

        @block.vector
        def _(dve):
            with dve.Fori(0, NBLK) as blk:
                with dve.Fori(0, TURNS) as turn:
                    for j in range(EPT):
                        x = blk * EA + turn * EPT + j
                        for h in range(HALVES):
                            n = 2 * x + h
                            dve.wait_ge(up_made, at(n + 1))
                            dve.wait_ge(silued, at(n + 1))
                            nc.vector.scalar_tensor_tensor(out=gated[h][:, :], in0=p_u[h][:, :],
                                                           scalar=raw[j][:, WCOLS + 1:WCOLS + 2], in1=silu[h][:, :],
                                                           op0=ALU.add, op1=ALU.mult).then_inc(steps, 1)
                            dve.wait_ge(w_in[j], dma_at(2 * (blk * TURNS + turn + 1)))
                            dve.wait_ge(split, at(n - 1))
                            dve.wait_ge(steps, at(2 * n + 1))
                            nc.vector.tensor_tensor(hid[h][:, :], gated[h][:, :], share[j][:, h * T:(h + 1) * T],
                                                    ALU.mult).then_inc(steps, 1)
                            dve.wait_ge(rounded, at(n + 1))
                            nc.vector.tensor_tensor(hid_lo[h][:, :], hid[h][:, :], hid_hi[h][:, :].bitcast(F32),
                                                    ALU.subtract).then_inc(split, 1)
                dve.wait_ge(res_in, dma_at(3 * blk + 3))
                for i in range(4):
                    two = slice(2 * i, 2 * i + 2)
                    dve.wait_ge(summed, at(2 * EA * blk + 2 * EA))
                    dve.wait_ge(out_ready, at(4 * blk))
                    nc.vector.tensor_tensor(scaled[:, two, :], p_o[i][:, :].rearrange("p (t n) -> p t n", n=D),
                                            gb[:, i // 2, :].unsqueeze(1).to_broadcast([P, 2, D]),
                                            ALU.mult).then_inc(scale_done, 1)

        @block.tensor
        def _(pe):
            def gate_up(n, j, h, blk):
                if h == 0:
                    pe.wait_ge(w_rounded, at(n // 2 + 1))
                    pe.wait_ge(w_split, at(n // 2 + 1))
                    pe.wait_ge(h_split, at(2 * blk + 2))
                for bank, made, c0, free, seen in ((p_g[h], gate_made, 0, silued, at(n - 1)),
                                                   (p_u[h], up_made, DC * I, steps, at(2 * n - 3))):
                    pe.wait_ge(free, seen)
                    prods = [(w, x, c) for w, x in ((w_hi, h_hi), (w_hi, h_lo), (w_lo, h_hi)) for c in range(DC)]
                    for k, (w, x, c) in enumerate(prods):
                        mm = nc.tensor.matmul(bank[:, :], w[j][:, c0 + c * I:c0 + (c + 1) * I],
                                              x[:, bass.ds(blk % 2 * PAR + h * DC + c, 1), :].squeeze(1),
                                              start=k == 0, stop=k == len(prods) - 1)
                    mm.then_inc(made, 1)

            def down(n, j, h):
                pe.wait_ge(rounded, at(n + 1))
                pe.wait_ge(split, at(n + 1))
                for t in range(TT):
                    tile = h * TT + t
                    o = p_o[tile // 2][:, tile % 2 * D:tile % 2 * D + D]
                    s, w0 = slice(t * P, (t + 1) * P), slice(2 * DC * I, WCOLS)
                    for x, w in ((hid_hi, w_hi), (hid_hi, w_lo), (hid_lo, w_hi)):
                        mm = nc.tensor.matmul(o, x[h][:, s], w[j][:, w0], start=False, stop=True,
                                              skip_group_check=True)
                mm.then_inc(summed, 1)

            for h in range(HALVES):
                gate_up(h, 0, h, 0)
            pe.wait_ge(bd_in, 16)
            with pe.Fori(0, NBLK) as blk:
                pe.wait_ge(wT_in, dma_at(blk + 1))
                for i in range(4):
                    pe.wait_ge(scale_done, at(4 * blk - 3 + i))
                    for t in (2 * i, 2 * i + 1):
                        mm = nc.tensor.matmul(p_o[i][:, t % 2 * D:t % 2 * D + D], wT[:, t * P:(t + 1) * P],
                                              bd[:, :], start=t % 2 == 0, stop=True, skip_group_check=True)
                    mm.then_inc(started, 1)
                with pe.Fori(0, TURNS) as turn:
                    for u in range(UNITS):
                        j, h = u // 2, u % 2
                        n = blk * (2 * EA) + turn * UNITS + u
                        down(n, j, h)
                        gate_up(n + 2, (j + 1) % EPT, h,
                                blk if u < UNITS - 2 else (blk * TURNS + turn + 1) // TURNS)


def build(nc, d):
    with ExitStack() as ctx:
        sb = lambda name, shape: ctx.enter_context(nc.sbuf_tensor(name, shape, F32))
        dram = lambda name, shape: nc.dram_tensor(name, shape, F32, kind="Internal").ap()
        d["qkbias"] = sb("qkbias", [P, 4])
        size = P + TT * P * PITCH + P
        d["scrC"] = dram("scrC", (4, size))
        d["scrP"] = dram("scrP", (4, size))
        d["tabs"] = dram("tabs", (PAIRS, P, 2, S))
        d["modrow"] = dram("modrow", (B, 6 * D))
        d["modcol"] = dram("modcol", (P, B, 6, DC))
        d["stack"] = dram("stack", (B * H, 2, 3 * DK, T))
        d["headpad"] = dram("headpad", (DK, T))
        d["vals"] = dram("vals", (B, P, PAIRS, TT * 2 * DKS))
        d["ctxd"] = dram("ctxd", (B * H, DKS, T))
        d["x1"] = dram("x1", (B, P, TT, D))
        d["h2T"] = dram("h2T", (B, P, DC, T))
        d["wT"] = dram("wT", (EA, B * T))
        build_setup(nc, d)
        build_qkv(nc, d)
        build_attention(nc, d)
        build_post(nc, d)
        build_experts(nc, d)


def laid_out(i):
    import numpy as np
    f = lambda k: np.asarray(i[k])
    a = {}
    a["x"] = f("L0_attn_x")
    for k in ("q", "k", "v", "o"):
        a["w" + k] = f("L0_attn_W" + k).T
    col = lambda v: v.reshape(DC, P).T
    a["bqk"] = np.stack([np.concatenate([col(f("L0_attn_bq")), col(f("L0_attn_bk"))], 1),
                         np.concatenate([col(f("L0_attn_bpq")), col(f("L0_attn_bpk"))], 1)], 2)
    a["bv"], a["bo"] = f("L0_attn_bv"), f("L0_attn_bo")

    def stacked(w):
        out = np.zeros((w.shape[0], H, 4, DK), w.dtype)
        out[:, :, 0:3] = w.reshape(w.shape[0], H, 1, DK)
        return out.reshape(w.shape[0], PAIRS * P)

    a["wpk"], a["wpq"] = stacked(f("L0_attn_Wpk").T), stacked(f("L0_attn_Wpq").T)
    a["wpos"] = np.concatenate([f("L0_attn_Wpq").T, f("L0_attn_Wpk").T], 1)
    a["bpos"] = np.stack([stacked(f(k)[None])[0].reshape(PAIRS, P).T
                          for k in ("L0_attn_bpk", "L0_attn_bpq")], 1)
    a["relT"] = f("L0_attn_rel_emb").T
    a["relTr"] = f("L0_attn_rel_emb")[::-1].T
    a["cT"] = f("L0_c").T
    a["wmod"] = f("L0_wmod")
    a["wr"], a["br"] = f("L0_ffn_Wr"), f("L0_ffn_br")

    def by_expert(routed, shared):
        return np.concatenate([f(routed), f(shared)[None]], 0)

    def rows(w):
        return w.reshape(EA, DC, P, -1).transpose(0, 2, 1, 3).reshape(EA, P, -1)

    a["wexp"] = np.concatenate([rows(by_expert("L0_ffn_Wg", "L0_ffn_Wg_s")), rows(by_expert("L0_ffn_Wu", "L0_ffn_Wu_s")),
                                by_expert("L0_ffn_Wd", "L0_ffn_Wd_s"),
                                by_expert("L0_ffn_bg", "L0_ffn_bg_s")[:, :, None],
                                by_expert("L0_ffn_bu", "L0_ffn_bu_s")[:, :, None]], 2)
    a["bd"] = by_expert("L0_ffn_bd", "L0_ffn_bd_s")
    a["ident"] = np.eye(P, dtype=np.float32)
    g = P // H
    a["spread"] = (np.eye(g)[None, :, :, None, None] * np.repeat(np.eye(H), DK, 1)
                   .reshape(H, 1, 1, DC, P)).reshape(P, g, DC, P).astype(np.float32)
    part = (np.arange(P) % 64) // DK
    row = np.arange(P) % 64
    hi1 = (part <= 1) | (row == 3 * DK)
    lo1 = (part == 2) | (row == 3 * DK + 1)
    hi2, lo2 = (part == 0) | (part == 2), part == 1
    mask = np.zeros((P, 4), np.float32)
    for k, (hi, lo) in enumerate(((hi1, lo1), (hi2, lo2))):
        mask[hi, 2 * k], mask[lo, 2 * k], mask[lo, 2 * k + 1] = 1.0, -1.0, 1.0
    a["rowmask"] = mask
    fsel = np.zeros((P, P), np.float32)
    for j in range(2):
        fsel[64 * j:64 * j + DK, 64 * j + 3 * DK:64 * j + 3 * DK + 2] = 1.0
    a["fsel"] = fsel
    a["pad"] = np.zeros((DK, T), np.float32)
    a["pad"][0:2] = 1.0
    r = np.arange(P)
    a["tri"] = np.stack([(r[None, :] < r[:, None]), (r[None, :] > r[:, None])], 1).astype(np.float32)
    return {k: np.ascontiguousarray(v) for k, v in a.items()}


def kernel(**inputs):
    import concourse.bacc as bacc
    from concourse.bass_utils import run_bass_kernel_spmd

    nc = bacc.Bacc("TRN2", target_bir_lowering=False, num_devices=1)
    arrays = laid_out(inputs)
    d = {k: nc.dram_tensor("in_" + k, v.shape, F32, kind="ExternalInput").ap() for k, v in arrays.items()}
    d["out"] = nc.dram_tensor("out", (B, T, D), F32, kind="ExternalOutput").ap()
    build(nc, d)
    r = run_bass_kernel_spmd(nc, [{"in_" + k: v for k, v in arrays.items()}], core_ids=[0])
    return r.results[0]["out"]
```
